# Optimizing a Trainium2 kernel written in Bass

```python
import numpy as np
import jax
import jax.numpy as jnp

def _softmax(x, axis=-1):
    return jax.nn.softmax(x, axis=axis)

def _gelu(x):
    return jax.nn.gelu(x, approximate=True)

def _silu(x):
    return jax.nn.silu(x)

def _sigmoid(x):
    return jax.nn.sigmoid(x)

def _layernorm(x, axis=-1, eps=1e-05):
    m = jnp.mean(x, axis=axis, keepdims=True)
    v = jnp.var(x, axis=axis, keepdims=True)
    return (x - m) / jnp.sqrt(v + eps)

def _scatter_add(tgt, idx, src, axis=0):
    return tgt.at[idx].add(src)

def _segment_sum(src, seg, n):
    return jax.ops.segment_sum(src, seg, n)
kernel_name = 'mk_flamingo_gated_d1_seqx_r4_268260'

def setup_inputs(seed: int=0):
    np.random.seed(seed)
    _w = jnp.asarray

    def _rec_inputs():
        import jax
        import jax.numpy as jnp
        _rk = jax.random.key(seed)
        x = -0.0002928 + 1 * jax.random.normal(jax.random.fold_in(_rk, 1), (16, 512, 256), jnp.float32)
        _lenS = 512 - jax.random.randint(jax.random.fold_in(_rk, 7), (16,), 0, max(1, 512 // 4) + 1, jnp.int32)
        _lenS2 = 1601 - jax.random.randint(jax.random.fold_in(_rk, 8), (16,), 0, max(1, 1601 // 4) + 1, jnp.int32)
        _ctx_1024P = jax.random.normal(jax.random.fold_in(_rk, 11), (16, 16, 256), jnp.float32)
        _ctx_1024c = jax.random.dirichlet(jax.random.fold_in(_rk, 511), 0.3 * jnp.ones((16,), jnp.float32), (16, 1601))
        _ctx_1024t = jnp.einsum('bsk,bkd->bsd', _ctx_1024c, _ctx_1024P)
        _ctx_1024t = _ctx_1024t * jax.lax.rsqrt(jnp.mean(jnp.square(_ctx_1024t)) + 1e-12) * 0.953939
        ctx_1024 = -1.39393e-06 + 0.999914 * (_ctx_1024t + 0.3 * jax.random.normal(jax.random.fold_in(_rk, 611), (16, 1601, 256), jnp.float32))
        _g = jax.random.normal(jax.random.fold_in(_rk, 9001), (2, 1), jnp.float32)
        _g = jnp.sign(_g) * jnp.maximum(jnp.abs(_g), 1.0) + (_g == 0) * 1.0
        g_xattn = _g[0]
        g_ffn = _g[1]
        return (x, ctx_1024, g_xattn, g_ffn)
    x, ctx_1024, g_xattn, g_ffn = _rec_inputs()

    def _L0_xattn_setup():
        import jax, jax.numpy as jnp
        import numpy as np
        D_MODEL = 256
        N_HEADS = 16
        HEAD_DIM = D_MODEL // N_HEADS

        def sparsemax(x):
            x = x - jnp.max(x, axis=-1, keepdims=True)
            zs = -jnp.sort(-x, axis=-1)
            L = x.shape[-1]
            rho = jnp.arange(1, L + 1, dtype=x.dtype)
            cssv = jnp.cumsum(zs, axis=-1) - 1.0
            support = zs > cssv / rho
            k = jnp.maximum(jnp.sum(support, axis=-1, keepdims=True), 1)
            tau = jnp.take_along_axis(cssv, k - 1, axis=-1) / k.astype(x.dtype)
            return jnp.clip(x - tau, 0.0)

        def _split_heads(x):
            B, L, _ = x.shape
            return x.reshape(B, L, N_HEADS, HEAD_DIM).transpose(0, 2, 1, 3)
        key = jax.random.key(seed)
        ks = jax.random.split(key, 11)
        B, L = (2, 512)
        s = 0.02
        inp = {'q': jax.random.normal(ks[0], (B, L, D_MODEL), jnp.float32), 'k': jax.random.normal(ks[1], (B, L, D_MODEL), jnp.float32), 'v': jax.random.normal(ks[2], (B, L, D_MODEL), jnp.float32), 'Wq': jax.random.normal(ks[3], (D_MODEL, D_MODEL), jnp.float32) * s, 'bq': jnp.zeros((D_MODEL,), jnp.float32), 'Wk': jax.random.normal(ks[4], (D_MODEL, D_MODEL), jnp.float32) * s, 'bk': jnp.zeros((D_MODEL,), jnp.float32), 'Wv': jax.random.normal(ks[5], (D_MODEL, D_MODEL), jnp.float32) * s, 'bv': jnp.zeros((D_MODEL,), jnp.float32), 'Wo': jax.random.normal(ks[6], (D_MODEL, D_MODEL), jnp.float32) * s, 'bo': jnp.zeros((D_MODEL,), jnp.float32)}
        return inp
    _L0_xattn_all = _L0_xattn_setup()
    _L0_xattn_in = {k: v for k, v in _L0_xattn_all.items() if k in ('Wq', 'bq', 'Wk', 'bk', 'Wv', 'bv', 'Wo', 'bo')}
    del _L0_xattn_all

    def _L0_ffn_setup():
        import jax, jax.numpy as jnp
        import numpy as np
        D, H, E, K = (256, 256, 8, 2)

        def _moe(x, router_w, w_in, b_in, w_out, b_out):
            B, S, Dm = x.shape
            T = B * S
            x2 = x.reshape(T, Dm)
            logits = x2 @ router_w
            probs = jax.nn.softmax(logits, axis=-1)
            top_p, top_e = jax.lax.top_k(probs, K)
            flat_e = top_e.reshape(-1)
            flat_p = top_p.reshape(-1)
            tok = jnp.repeat(jnp.arange(T), K)
            order = jnp.argsort(flat_e)
            se, sp, st = (flat_e[order], flat_p[order], tok[order])
            xd = x2[st]
            N = xd.shape[0]
            h = jnp.zeros((N, H), x.dtype)
            for e in range(E):
                m = (se == e)[:, None]
                h = h + jnp.where(m, jax.nn.gelu(xd @ w_in[e] + b_in[e]), 0.0)
            y = jnp.zeros((N, Dm), x.dtype)
            for e in range(E):
                m = (se == e)[:, None]
                y = y + jnp.where(m, h @ w_out[e] + b_out[e], 0.0)
            y = y * sp[:, None]
            out = jnp.zeros((T, Dm), x.dtype).at[st].add(y)
            return out.reshape(B, S, Dm)
        key = jax.random.key(seed)
        ks = jax.random.split(key, 5)
        s = lambda k, shape, scale: jax.random.normal(k, shape, dtype=jnp.float32) * scale
        return {'input_batch': s(ks[0], (2, 128, D), 1.0), 'router_w': s(ks[1], (D, E), D ** (-0.5)), 'w_in': s(ks[2], (E, D, H), D ** (-0.5)), 'b_in': jnp.zeros((E, H), jnp.float32), 'w_out': s(ks[3], (E, H, D), H ** (-0.5)), 'b_out': jnp.zeros((E, D), jnp.float32)}
    _L0_ffn_all = _L0_ffn_setup()
    _L0_ffn_in = {k: v for k, v in _L0_ffn_all.items() if k in ('router_w', 'w_in', 'b_in', 'w_out', 'b_out')}
    del _L0_ffn_all
    return {'x': x, 'ctx_1024': ctx_1024, 'g_xattn': g_xattn, 'g_ffn': g_ffn, 'L0_xattn_Wq': _L0_xattn_in['Wq'], 'L0_xattn_bq': _L0_xattn_in['bq'], 'L0_xattn_Wk': _L0_xattn_in['Wk'], 'L0_xattn_bk': _L0_xattn_in['bk'], 'L0_xattn_Wv': _L0_xattn_in['Wv'], 'L0_xattn_bv': _L0_xattn_in['bv'], 'L0_xattn_Wo': _L0_xattn_in['Wo'], 'L0_xattn_bo': _L0_xattn_in['bo'], 'L0_ffn_router_w': _L0_ffn_in['router_w'], 'L0_ffn_w_in': _L0_ffn_in['w_in'], 'L0_ffn_b_in': _L0_ffn_in['b_in'], 'L0_ffn_w_out': _L0_ffn_in['w_out'], 'L0_ffn_b_out': _L0_ffn_in['b_out']}

def reference(x, ctx_1024, g_xattn, g_ffn, L0_xattn_Wq, L0_xattn_bq, L0_xattn_Wk, L0_xattn_bk, L0_xattn_Wv, L0_xattn_bv, L0_xattn_Wo, L0_xattn_bo, L0_ffn_router_w, L0_ffn_w_in, L0_ffn_b_in, L0_ffn_w_out, L0_ffn_b_out):
    import jax
    import jax.numpy as jnp

    def _L0_xattn_ref(q, k, v, Wq, bq, Wk, bk, Wv, bv, Wo, bo):
        import jax, jax.numpy as jnp
        import numpy as np
        D_MODEL = 256
        N_HEADS = 16
        HEAD_DIM = D_MODEL // N_HEADS

        def sparsemax(x):
            x = x - jnp.max(x, axis=-1, keepdims=True)
            zs = -jnp.sort(-x, axis=-1)
            L = x.shape[-1]
            rho = jnp.arange(1, L + 1, dtype=x.dtype)
            cssv = jnp.cumsum(zs, axis=-1) - 1.0
            support = zs > cssv / rho
            k = jnp.maximum(jnp.sum(support, axis=-1, keepdims=True), 1)
            tau = jnp.take_along_axis(cssv, k - 1, axis=-1) / k.astype(x.dtype)
            return jnp.clip(x - tau, 0.0)

        def _split_heads(x):
            B, L, _ = x.shape
            return x.reshape(B, L, N_HEADS, HEAD_DIM).transpose(0, 2, 1, 3)
        qh = _split_heads(q @ Wq + bq)
        kh = _split_heads(k @ Wk + bk)
        vh = _split_heads(v @ Wv + bv)
        scale = HEAD_DIM ** (-0.5)
        scores = jnp.einsum('bhqd,bhkd->bhqk', qh, kh) * scale
        attn = sparsemax(scores)
        out = jnp.einsum('bhqk,bhkd->bhqd', attn, vh)
        B, L = (q.shape[0], q.shape[1])
        out = out.transpose(0, 2, 1, 3).reshape(B, L, D_MODEL)
        return out @ Wo + bo

    def _L0_ffn_ref(input_batch, router_w, w_in, b_in, w_out, b_out):
        import jax, jax.numpy as jnp
        import numpy as np
        D, H, E, K = (256, 256, 8, 2)

        def _moe(x, router_w, w_in, b_in, w_out, b_out):
            B, S, Dm = x.shape
            T = B * S
            x2 = x.reshape(T, Dm)
            logits = x2 @ router_w
            probs = jax.nn.softmax(logits, axis=-1)
            top_p, top_e = jax.lax.top_k(probs, K)
            flat_e = top_e.reshape(-1)
            flat_p = top_p.reshape(-1)
            tok = jnp.repeat(jnp.arange(T), K)
            order = jnp.argsort(flat_e)
            se, sp, st = (flat_e[order], flat_p[order], tok[order])
            xd = x2[st]
            N = xd.shape[0]
            h = jnp.zeros((N, H), x.dtype)
            for e in range(E):
                m = (se == e)[:, None]
                h = h + jnp.where(m, jax.nn.gelu(xd @ w_in[e] + b_in[e]), 0.0)
            y = jnp.zeros((N, Dm), x.dtype)
            for e in range(E):
                m = (se == e)[:, None]
                y = y + jnp.where(m, h @ w_out[e] + b_out[e], 0.0)
            y = y * sp[:, None]
            out = jnp.zeros((T, Dm), x.dtype).at[st].add(y)
            return out.reshape(B, S, Dm)
        return _moe(input_batch, router_w, w_in, b_in, w_out, b_out)
    x = x + jnp.tanh(g_xattn[0]) * _L0_xattn_ref(_layernorm(x, axis=-1), ctx_1024, ctx_1024, L0_xattn_Wq, L0_xattn_bq, L0_xattn_Wk, L0_xattn_bk, L0_xattn_Wv, L0_xattn_bv, L0_xattn_Wo, L0_xattn_bo)
    x = x + jnp.tanh(g_ffn[0]) * _L0_ffn_ref(_layernorm(x, axis=-1), L0_ffn_router_w, L0_ffn_w_in, L0_ffn_b_in, L0_ffn_w_out, L0_ffn_b_out)
    return x

_drawn_inputs = setup_inputs


def setup_inputs(seed=0):
    import zlib

    import numpy as np

    out = dict(_drawn_inputs(seed))
    spreads = {'L0_xattn_bq': (0.0, 0.1),
     'L0_xattn_bk': (0.0, 0.8),
     'L0_xattn_bv': (0.0, 0.1),
     'L0_xattn_bo': (0.0, 0.1),
     'L0_ffn_b_in': (0.0, 0.291),
     'L0_ffn_b_out': (0.0, 0.1)}
    factors = {}
    for name, (base, spread) in spreads.items():
        noise = np.random.default_rng([zlib.crc32(name.encode()), seed]).standard_normal(out[name].shape)
        drawn = base * np.exp(spread * noise) if base else spread * noise
        out[name] = jnp.asarray(drawn.astype(out[name].dtype))
    for name, factor in factors.items():
        out[name] = (out[name] * factor).astype(out[name].dtype)
    return out
```

```python
from contextlib import ExitStack

import concourse.bass as bass
from concourse import mybir

F32 = mybir.dt.float32
BF16 = mybir.dt.bfloat16
I32 = mybir.dt.int32
U32 = mybir.dt.uint32
ALU = mybir.AluOpType
ACT = mybir.ActivationFunctionType
AX = mybir.AxisListType

P = 128
BATCH, QUERIES, KEYS, DIM = 16, 512, 1601, 256
HEADS, HEAD_DIM = 16, 16
EXPERTS, HIDDEN = 8, 256
SCALE = HEAD_DIM ** -0.5
EPS = 1e-5
HALVES = DIM // P
TILES = QUERIES // P
KCHUNKS = -(-KEYS // P)
LAST_KEYS = KEYS - (KCHUNKS - 1) * P
BANK = 512
KEY_PIECES = [(c, min(c + BANK, KEYS)) for c in range(0, KEYS, BANK)]

K_PARTS = [0, 1, 2, 0, 1, 0]
Q_PARTS = [0, 0, 0, 1, 1, 2]
GROUPS = len(K_PARTS)
SCORE_ROWS = GROUPS * HEAD_DIM
TAU_ROWS = 3

CHUNKS = 36
RUNS = [(KEYS * c // CHUNKS, KEYS * (c + 1) // CHUNKS) for c in range(CHUNKS)]
CAND = CHUNKS * 8
FIRST, SECOND = 2, 5
ROUNDS = 4
EXACT = 3e-5
SETTLED = 3e-7
GENERAL_STEPS = 26


def project_program(nc, x, ctx_t, wq, bq, wk, bk, wv, bv, ident_in, q_parts, k_parts, v_heads):
    with ExitStack() as ctx:
        def sb(name, shape, dt=F32):
            return ctx.enter_context(nc.sbuf_tensor("p_" + name, shape, dt))

        def sem(name):
            return ctx.enter_context(nc.semaphore("p_" + name))

        RING = 5
        ring = ctx.enter_context(nc.psum_tensor("p_ring", [P, RING, BANK], F32))
        xt = sb("x", [P, 2, TILES, DIM])
        ct = sb("ctx", [P, 2, HALVES, KEYS])
        wq_s, wk_s, wv_s = (sb(n, [P, HALVES, DIM]) for n in ("wq", "wk", "wv"))
        bq_s, bk_s = sb("bq", [P, HALVES]), sb("bk", [P, HALVES])
        bqs = sb("bqs", [P, HALVES])
        bv_s = sb("bv", [P, DIM])
        ident = sb("ident", [P, P])
        stats = sb("stats", [P, TILES, 6])
        moments = sb("moments", [P, TILES, 2])
        std = sb("std", [P, TILES])
        veps = sb("veps", [P, TILES])
        rstd = sb("rstd", [P, TILES])
        fix = sb("fix", [P, TILES])
        xn = sb("xn", [P, TILES, DIM])
        xnt = sb("xnt", [P, HALVES, QUERIES])
        qf = sb("qf", [P, HALVES, QUERIES])
        qr = sb("qr", [P, HALVES, QUERIES])
        qs = sb("qs", [P, 3, HALVES, QUERIES], BF16)
        kf = sb("kf", [P, HALVES, KEYS])
        kr = sb("kr", [P, HALVES, KEYS])
        ks = sb("ks", [P, 3, HALVES, KEYS], BF16)
        vt = sb("v", [P, HEADS, KCHUNKS, HEAD_DIM])

        weights = sem("weights")
        x_loaded = [sem("x_loaded0"), sem("x_loaded1")]
        ctx_loaded = [sem("ctx_loaded0"), sem("ctx_loaded1")]
        stats_done = sem("stats_done")
        std_done = sem("std_done")
        chain = sem("chain")
        normed = sem("normed")
        job_made = sem("job_made")
        job_used = sem("job_used")
        job_used_dve = sem("job_used_dve")
        passed, passed_sp = sem("passed"), sem("passed_sp")
        q_rest = sem("q_rest")
        k_rest = sem("k_rest")
        q_split = sem("q_split")
        k_split = sem("k_split")
        q_high = sem("q_high")
        k_high = sem("k_high")
        q_mid = sem("q_mid")
        k_mid = sem("k_mid")
        q_stored = sem("q_stored")
        k_stored = sem("k_stored")
        v_stored = sem("v_stored")
        consts = sem("consts")

        jobs = [("turn", a) for a in range(HALVES)]
        jobs += [("k", a, c) for a in range(HALVES) for c in range(len(KEY_PIECES))]
        jobs += [("q", a) for a in range(HALVES)]
        jobs += [("v", c) for c in range(KCHUNKS)]
        NJ = len(jobs)
        assert NJ % RING == 0
        by_dve = [j[0] in ("turn", "v") for j in jobs]
        dve_jobs, act_jobs = sum(by_dve), NJ - sum(by_dve)

        def readers_before(b, n):
            return b * dve_jobs + sum(by_dve[:n]), b * act_jobs + n - sum(by_dve[:n])

        block = ctx.enter_context(nc.Block())

        @block.sync
        def _(sp):
            for dst, src in ((wq_s, wq), (wk_s, wk), (wv_s, wv)):
                sp.dma_start(dst[:], src.rearrange("(a p) n -> p a n", p=P)).then_inc(weights, 16)
            for dst, src in ((bq_s, bq), (bk_s, bk)):
                for a in range(HALVES):
                    sp.dma_start(dst[:, a:a + 1], src[a * P:(a + 1) * P].rearrange("(p o) -> p o", o=1)).then_inc(weights, 16)
            sp.dma_start(bv_s[:], bv.rearrange("(o n) -> o n", o=1).broadcast_to([P, DIM])).then_inc(weights, 16)
            sp.dma_start(ident[:], ident_in).then_inc(weights, 16)

            def load(b, u, first):
                if not first:
                    sp.wait_ge(normed, TILES * (b - 1))
                    sp.sem_inc(passed_sp, 1)
                    sp.wait_ge(job_made, NJ * (b - 1))
                    sp.sem_inc(passed_sp, 1)
                sp.dma_start(xt[:, u], x[b].rearrange("(t p) d -> p t d", p=P)).then_inc(x_loaded[u], 16)
                sp.dma_start(ct[:, u], ctx_t[b].rearrange("(a p) n -> p a n", p=P)).then_inc(ctx_loaded[u], 16)

            def store(b):
                sp.wait_ge(q_split, b + 1)
                for s in range(3):
                    sp.dma_start(q_parts[s, bass.ds(b * DIM, DIM)].rearrange("(a p) n -> p a n", p=P), qs[:, s]).then_inc(q_stored, 16)
                sp.wait_ge(k_split, b + 1)
                for s in range(3):
                    sp.dma_start(k_parts[s, bass.ds(b * DIM, DIM)].rearrange("(a p) n -> p a n", p=P), ks[:, s]).then_inc(k_stored, 16)
                sp.wait_ge(job_used_dve, dve_jobs * (b + 1))
                sp.dma_start(v_heads[bass.ds(b * HEADS, HEADS)].rearrange("h p c d -> p h c d")[:, :, 0:KCHUNKS - 1], vt[:, :, 0:KCHUNKS - 1]).then_inc(v_stored, 16)
                sp.dma_start(v_heads[bass.ds(b * HEADS, HEADS)].rearrange("h p c d -> p h c d")[0:LAST_KEYS, :, KCHUNKS - 1:], vt[0:LAST_KEYS, :, KCHUNKS - 1:]).then_inc(v_stored, 16)

            load(0, 0, True)
            load(1, 1, True)
            if BATCH > 2:
                with sp.Fori(0, BATCH // 2 - 1) as g:
                    for u in range(2):
                        store(2 * g + u)
                        load(2 * g + u + 2, u, False)
            for b in range(BATCH - 2, BATCH):
                store(b)
            sp.wait_ge(q_stored, 16 * 3 * BATCH)
            sp.wait_ge(k_stored, 16 * 3 * BATCH)
            sp.wait_ge(v_stored, 16 * 2 * BATCH)

        @block.tensor
        def _(pe):
            pe.wait_ge(weights, 16 * 9)
            def pair(g):
                for u in range(2):
                    b = 2 * g + u
                    pe.wait_ge(normed, TILES * (b + 1))
                    for n, job in enumerate(jobs):
                        bank = ring[:, n % RING]
                        if n >= RING:
                            by, m = by_dve[n - RING], n - RING
                            d, a = readers_before(b, m + 1)
                            pe.wait_ge(job_used_dve if by else job_used, d if by else a)
                        elif not isinstance(b, int) or b > 0:
                            m = NJ + n - RING
                            by = by_dve[m]
                            d, a = readers_before(b, m + 1)
                            with_prev = (d - dve_jobs) if by else (a - act_jobs)
                            pe.wait_ge(job_used_dve if by else job_used, with_prev)
                        if job[0] == "turn":
                            a = job[1]
                            for t in range(TILES):
                                mm = nc.tensor.transpose(bank[:, t * P:(t + 1) * P], xn[:, t, a * P:(a + 1) * P], ident[:])
                        elif job[0] == "q":
                            if job[1] == 0:
                                pe.wait_ge(job_used_dve, b * dve_jobs + HALVES)
                            for c in range(HALVES):
                                mm = nc.tensor.matmul(bank, wq_s[:, c, job[1] * P:(job[1] + 1) * P], xnt[:, c], start=c == 0, stop=c == HALVES - 1)
                        elif job[0] == "k":
                            if job[1:] == (0, 0):
                                pe.wait_ge(ctx_loaded[u], 16 * (g + 1))
                            lo, hi = KEY_PIECES[job[2]]
                            for c in range(HALVES):
                                mm = nc.tensor.matmul(bank[:, 0:hi - lo], wk_s[:, c, job[1] * P:(job[1] + 1) * P], ct[:, u, c, lo:hi], start=c == 0, stop=c == HALVES - 1)
                        else:
                            lo, hi = job[1] * P, min(job[1] * P + P, KEYS)
                            for c in range(HALVES):
                                mm = nc.tensor.matmul(bank[0:hi - lo, 0:DIM], ct[:, u, c, lo:hi], wv_s[:, c], start=c == 0, stop=c == HALVES - 1)
                        mm.then_inc(job_made, 1)

            pair(0)
            with pe.Fori(1, BATCH // 2) as g:
                pair(g)

        @block.scalar
        def _(act):
            act.wait_ge(weights, 16 * 9)
            nc.scalar.mul(bqs[:], bq_s[:], SCALE).then_inc(consts, 1)
            act.wait_ge(consts, 1)
            with act.Fori(0, BATCH) as b:
                act.wait_ge(stats_done, b + 1)
                nc.scalar.activation(std[:], veps[:], ACT.Sqrt).then_inc(std_done, 1)
                for n, job in enumerate(jobs):
                    if job[0] == "k":
                        a, c = job[1:]
                        if (a, c) == (0, 0):
                            act.wait_ge(k_rest, b)
                        lo, hi = KEY_PIECES[c]
                        act.wait_ge(job_made, NJ * b + n + 1)
                        nc.scalar.activation(kf[:, a, lo:hi], ring[:, n % RING, 0:hi - lo], ACT.Identity, bias=bk_s[:, a:a + 1]).then_inc(job_used, 1)
                        if (a, c) == (HALVES - 1, len(KEY_PIECES) - 1):
                            act.wait_ge(job_used, readers_before(b, n + 1)[1])
                            act.wait_ge(k_stored, 48 * b)
                            nc.scalar.copy(ks[:, 0], kf[:]).then_inc(k_high, 1)
                    elif job[0] == "q":
                        a = job[1]
                        if a == 0:
                            act.wait_ge(q_rest, b)
                        act.wait_ge(job_made, NJ * b + n + 1)
                        nc.scalar.activation(qf[:, a], ring[:, n % RING], ACT.Identity, bias=bqs[:, a:a + 1], scale=SCALE).then_inc(job_used, 1)
                        if a == HALVES - 1:
                            act.wait_ge(job_used, readers_before(b, n + 1)[1])
                            act.wait_ge(q_stored, 48 * b)
                            nc.scalar.copy(qs[:, 0], qf[:]).then_inc(q_high, 1)

        @block.gpsimd
        def _(pool):
            with pool.Fori(0, BATCH) as b:
                pool.wait_ge(k_high, b + 1)
                pool.wait_ge(k_split, b)
                nc.gpsimd.tensor_tensor(kr[:], kf[:], ks[:, 0], ALU.subtract).then_inc(k_rest, 1)
                pool.wait_ge(q_high, b + 1)
                pool.wait_ge(q_split, b)
                nc.gpsimd.tensor_tensor(qr[:], qf[:], qs[:, 0], ALU.subtract).then_inc(q_rest, 1)

        @block.vector
        def _(dve):
            dve.wait_ge(weights, 16 * 9)
            LINKS = 5 + 2

            def batch(b, u, g):
                made = [LINKS * b]

                def link(ins):
                    made[0] = made[0] + 1
                    ins.then_inc(chain, 1)
                    dve.wait_ge(chain, made[0])

                dve.wait_ge(x_loaded[u], 16 * (g + 1))
                for t in range(TILES):
                    ins = nc.vector.bn_stats(stats[:, t], xt[:, u, t])
                link(ins)
                dve.sem_inc(passed, 1)
                for t in range(TILES):
                    ins = nc.vector.bn_aggr(moments[:, t], stats[:, t])
                link(ins)
                nc.vector.tensor_scalar(veps[:], moments[:, :, 1], EPS, None, ALU.add).then_inc(stats_done, 1)
                dve.wait_ge(std_done, b + 1)
                link(nc.vector.reciprocal(rstd[:], std[:]))
                link(nc.vector.tensor_tensor(fix[:], rstd[:], rstd[:], ALU.mult))
                link(nc.vector.tensor_tensor(fix[:], fix[:], veps[:], ALU.mult))
                link(nc.vector.tensor_scalar(fix[:], fix[:], -0.5, 1.5, ALU.mult, ALU.add))
                link(nc.vector.tensor_tensor(rstd[:], rstd[:], fix[:], ALU.mult))
                for t in range(TILES):
                    nc.vector.tensor_scalar(xn[:, t], xt[:, u, t], moments[:, t, 0:1], rstd[:, t:t + 1], ALU.subtract, ALU.mult).then_inc(normed, 1)
                for n, job in enumerate(jobs):
                    if job[0] == "turn":
                        if job[1] == 0:
                            dve.wait_ge(q_high, b)
                        dve.wait_ge(job_made, NJ * b + n + 1)
                        nc.vector.tensor_copy(xnt[:, job[1]], ring[:, n % RING]).then_inc(job_used_dve, 1)
                for n, job in enumerate(jobs):
                    if job[0] == "v":
                        c = job[1]
                        rows = P if c < KCHUNKS - 1 else LAST_KEYS
                        if c == 0:
                            dve.wait_ge(v_stored, 32 * b)
                        dve.wait_ge(job_made, NJ * b + n + 1)
                        nc.vector.tensor_tensor(vt[0:rows, :, c, :], ring[0:rows, n % RING, 0:DIM].rearrange("p (h d) -> p h d", h=HEADS),
                                                bv_s[0:rows].rearrange("p (h d) -> p h d", h=HEADS), ALU.add).then_inc(job_used_dve, 1)
                for rest, high, mid, split, r, s in ((q_rest, q_high, q_mid, q_split, qr, qs), (k_rest, k_high, k_mid, k_split, kr, ks)):
                    dve.wait_ge(rest, b + 1)
                    nc.vector.tensor_copy(s[:, 1], r[:]).then_inc(mid, 1)
                    dve.wait_ge(mid, b + 1)
                    nc.vector.tensor_tensor(s[:, 2], r[:], s[:, 1], ALU.subtract).then_inc(split, 1)

            with dve.Fori(0, BATCH // 2) as g:
                for u in range(2):
                    batch(2 * g + u, u, g)


def attend_program(nc, q_parts, k_parts, v_heads, ident_in, o_parts):
    N = BATCH * HEADS
    U = 6
    SLOTS = 3
    RING = 3
    LAG = 3
    S_PIECES = [(t, lo, min(lo + 2 * BANK, KEYS)) for t in range(TILES) for lo in range(0, KEYS, 2 * BANK)]
    T_PIECES = [range(c, min(c + 2, KCHUNKS)) for c in range(0, KCHUNKS, 2)]
    NS, NT = len(S_PIECES), len(T_PIECES)
    assert (NS + NT) % RING == 0 and U % SLOTS == 0 and U % 2 == 0

    def groups(do_s, do_t):
        place, out = 0, []
        for g in range(TILES):
            own = []
            for kind, n, there in [("s", 2 * g, do_s), ("s", 2 * g + 1, do_s)] + [("t", k, do_t) for k in range(2 * g, min(2 * g + 2, NT))]:
                if there:
                    own.append((kind, n, place))
                    place += 1
            out.append(own)
        return out

    def before(i):
        if isinstance(i, int):
            return NS * min(i, N) + NT * min(max(0, i - LAG), N)
        return i * (NS + NT) - NT * LAG

    def slot(i, place):
        return ((before(i) if isinstance(i, int) else -NT * LAG) + place) % RING

    def score_place(n, do_t):
        return next(p for own in groups(True, do_t) for kind, m, p in own if kind == "s" and m == n)

    def walk(engine, step):
        for i in range(U):
            step(i, i)
        with engine.Fori(1, N // U) as g:
            for u in range(U):
                step(g * U + u, u)
        for i in range(N // U * U, N + LAG + 1):
            step(i, i % U)

    def has(i, lag):
        return not isinstance(i, int) or 0 <= i - lag < N

    with ExitStack() as ctx:
        def sb(name, shape, dt=F32):
            return ctx.enter_context(nc.sbuf_tensor("a_" + name, shape, dt))

        def sem(name):
            return ctx.enter_context(nc.semaphore("a_" + name))

        ring = ctx.enter_context(nc.psum_tensor("a_ring", [P, RING, 2 * BANK], F32))
        out_ps = ctx.enter_context(nc.psum_tensor("a_out", [P, BANK], F32))
        turn_ps = ctx.enter_context(nc.psum_tensor("a_turn", [P, BANK], F32))

        k_st = sb("k", [P, U, KEYS], BF16)
        q_st = sb("q", [P, U, QUERIES], BF16)
        v_st = sb("v", [P, U, KCHUNKS, HEAD_DIM])
        scores = sb("scores", [P, SLOTS, TILES, KEYS])
        attn = sb("attn", [P, NT, 2 * BANK])
        o_sb = sb("o", [P, QUERIES])
        cand = sb("cand", [P, SLOTS, TILES, CHUNKS, 8])
        junk = sb("junk", [P, KEYS])
        junk_act = sb("junk_act", [P, TILES, CAND])
        zeros = sb("zeros", [P, 1])
        ident_f = sb("ident_f", [P, P])
        ident = sb("ident", [P, P], BF16)
        ones = sb("ones", [P, 1], BF16)
        tau = sb("tau", [P, TILES])
        top = sb("top", [P, TILES])
        ntau = sb("ntau", [P, TILES])
        excess = sb("excess", [P, TILES])
        own_excess = sb("own_excess", [P, TILES])
        count = sb("count", [P, TILES])
        inv = sb("inv", [P, TILES])
        move = sb("move", [P, TILES])
        w1 = sb("w1", [P, TILES])
        w2 = sb("w2", [P, TILES])
        bad = sb("bad", [P, TILES], BF16)
        bad_i = sb("bad_i", [1, TILES + 1], I32)
        found = sb("found", [P, TILES])
        g_excess, g_count, g1, g2 = (sb(n, [P, TILES]) for n in ("g_excess", "g_count", "g1", "g2"))
        neg = sb("neg", [P, TILES])
        split = sb("split", [P, TILES, TAU_ROWS], BF16)
        flag = sb("flag", [P, 32])
        flag_t = sb("flag_t", [P, 32])
        flag_i = sb("flag_i", [P, 1], I32)

        loaded = [sem(f"loaded{u}") for u in range(U)]
        ident_loaded = sem("ident_loaded")
        setup = sem("setup")
        piece_made = sem("piece_made")
        piece_used = sem("piece_used")
        products = sem("products")
        out_copied = sem("out_copied")
        out_stored = sem("out_stored")
        cand_made = sem("cand_made")
        tau_tried = sem("tau_tried")
        excess_made = sem("excess_made")
        bad_ready = sem("bad_ready")
        bad_counted = sem("bad_counted")
        tau_split = sem("tau_split")
        tau_turned = sem("tau_turned")
        tau_in_q = sem("tau_in_q")
        chain = sem("chain")
        passed = sem("passed")
        general = sem("general")
        SETUP = 5
        LOADS = len(K_PARTS) + len(Q_PARTS) + 2

        block = ctx.enter_context(nc.Block())

        @block.sync
        def _(sp):
            sp.dma_start(ident_f[:], ident_in).then_inc(ident_loaded, 16)

            def load(i, u):
                for parts, st, run in ((K_PARTS, k_st, k_parts), (Q_PARTS, q_st, q_parts)):
                    for n, s in enumerate(parts):
                        sp.dma_start(st[n * HEAD_DIM:(n + 1) * HEAD_DIM, u], run[s, bass.ds(i * HEAD_DIM, HEAD_DIM)]).then_inc(loaded[u], 16)
                sp.dma_start(v_st[:, u, 0:KCHUNKS - 1], v_heads[i][:, 0:KCHUNKS - 1]).then_inc(loaded[u], 16)
                sp.dma_start(v_st[0:LAST_KEYS, u, KCHUNKS - 1:], v_heads[i][0:LAST_KEYS, KCHUNKS - 1:]).then_inc(loaded[u], 16)

            def store(i):
                sp.wait_ge(out_copied, i + 1)
                for s in range(4):
                    sp.dma_start(o_parts[s, bass.ds(i * HEAD_DIM, HEAD_DIM)], o_sb[32 * s:32 * s + HEAD_DIM]).then_inc(out_stored, 16)

            for i in range(U):
                load(i, i)
            with sp.Fori(0, N // U - 1) as g:
                for u in range(U):
                    i = g * U + u
                    sp.wait_ge(products, NT * (i + 1))
                    load(i + U, u)
                    store(i)
            for i in range((N // U - 1) * U, N):
                if i + U < N:
                    sp.wait_ge(products, NT * (i + 1))
                    load(i + U, i % U)
                store(i)
            sp.wait_ge(out_stored, 64 * N)

        @block.tensor
        def _(pe):
            pe.wait_ge(setup, SETUP)

            def multiply(i, k, u, t_place):
                pe.wait_ge(piece_used, t_place + 1)
                if k == 0:
                    pe.wait_ge(out_copied, i)
                for c in T_PIECES[k]:
                    rows = P if c < KCHUNKS - 1 else LAST_KEYS
                    at = 32 * (c % 4)
                    mm = nc.tensor.matmul(out_ps[at:at + HEAD_DIM], v_st[0:rows, u, c], attn[0:rows, k, (c % 2) * BANK:(c % 2 + 1) * BANK],
                                          start=c < 4, stop=c >= KCHUNKS - 4)
                mm.then_inc(products, 1)

            group_now = [None]

            def i_group(i, u):
                return group_now[0]

            def before_prev(i):
                return before(i - 1) if isinstance(i, int) else before(i) - NS - NT

            def count_bad(i):
                pe.wait_ge(bad_ready, i + 1)
                nc.tensor.matmul(turn_ps[0:1, 0:TILES], ones[:], bad[:], start=True, stop=True)
                for t in range(TILES):
                    mm = nc.tensor.matmul(turn_ps[0:1, TILES:TILES + 1], ones[:], bad[:, t:t + 1], start=t == 0, stop=t == TILES - 1)
                mm.then_inc(bad_counted, 1)

            def turn_tau(i):
                pe.wait_ge(tau_split, i + 1)
                if not isinstance(i, int) or i >= 1:
                    pe.wait_ge(tau_in_q, i)
                for t in range(TILES):
                    mm = nc.tensor.matmul(turn_ps[SCORE_ROWS:SCORE_ROWS + TAU_ROWS, t * P:(t + 1) * P], split[:, t], ident[:], start=True, stop=True)
                mm.then_inc(tau_turned, 1)

            def step(i, u):
                do_s, do_t = has(i, 0), has(i, LAG)
                ut = (u - LAG) % U
                if do_s:
                    pe.wait_ge(loaded[u], 16 * LOADS * ((i // U if isinstance(i, int) else i_group(i, u)) + 1))
                if do_t:
                    pe.wait_ge(tau_in_q, i - LAG + 1)
                order = groups(do_s, do_t)
                for g, own in enumerate(order):
                    for kind, n, place in own:
                        seq = before(i) + place
                        if not isinstance(i, int) or seq >= RING:
                            pe.wait_ge(piece_used, seq - RING + 1)
                        at = ring[:, slot(i, place)]
                        if kind == "s":
                            t, lo, hi = S_PIECES[n]
                            for c in range(lo, hi, BANK):
                                w = min(BANK, hi - c)
                                mm = nc.tensor.matmul(at[:, c - lo:c - lo + w], q_st[0:SCORE_ROWS, u, t * P:(t + 1) * P], k_st[0:SCORE_ROWS, u, c:c + w], start=True, stop=True)
                        else:
                            for m, c in enumerate(T_PIECES[n]):
                                rows = P if c < KCHUNKS - 1 else LAST_KEYS
                                mm = nc.tensor.matmul(at[0:rows, m * BANK:(m + 1) * BANK], k_st[0:SCORE_ROWS + TAU_ROWS, ut, c * P:c * P + rows],
                                                      q_st[0:SCORE_ROWS + TAU_ROWS, ut], start=True, stop=True)
                        mm.then_inc(piece_made, 1)
                    if g == 0:
                        if has(i, LAG + 1):
                            last = NT - 1
                            p = next(p for o in groups(has(i, 1), has(i, LAG + 1)) for kd, n, p in o if (kd, n) == ("t", last))
                            multiply(i - LAG - 1, last, (ut - 1) % U, before_prev(i) + p)
                    else:
                        for kd, n, p in order[g - 1]:
                            if kd == "t":
                                multiply(i - LAG, n, ut, before(i) + p)
                    if g == 2 and has(i, 2):
                        count_bad(i - 2)
                    if g == 3 and has(i, 2):
                        turn_tau(i - 2)
            for i in range(U):
                step(i, i)
            with pe.Fori(1, N // U) as g:
                group_now[0] = g
                for u in range(U):
                    step(g * U + u, u)
            for i in range(N // U * U, N + LAG + 1):
                step(i, i % U)

        @block.scalar
        def _(act):
            act.wait_ge(setup, SETUP)

            def measure_excess(i, slot, r):
                act.wait_ge(tau_tried, ROUNDS * i + r + 1)
                for t in range(TILES):
                    w = SECOND if r == 0 else 8
                    ins = nc.scalar.activation(junk_act[:, t, 0:CHUNKS * w].rearrange("p (a b) -> p a b", a=CHUNKS), cand[:, slot, t, :, 0:w], ACT.Relu,
                                               bias=ntau[:, t:t + 1], accum_out=excess[:, t:t + 1])
                ins.then_inc(excess_made, 1)

            def step(i, u):
                do_s, do_t = has(i, 0), has(i, LAG)
                ut = (u - LAG) % U
                if do_t:
                    act.wait_ge(tau_turned, i - LAG + 1)
                    nc.scalar.copy(q_st[SCORE_ROWS:SCORE_ROWS + TAU_ROWS, ut], turn_ps[SCORE_ROWS:SCORE_ROWS + TAU_ROWS]).then_inc(tau_in_q, 1)
                if do_s and (not isinstance(i, int) or i >= SLOTS):
                    act.wait_ge(tau_split, i - SLOTS + 1)
                for g, own in enumerate(groups(do_s, do_t)):
                    for kind, n, place in own:
                        seq = before(i) + place
                        at = ring[:, slot(i, place)]
                        if kind == "t" and (not isinstance(i, int) or i > LAG):
                            act.wait_ge(products, NT * (i - LAG - 1) + n + 1)
                        act.wait_ge(piece_made, seq + 1)
                        if kind == "s":
                            t, lo, hi = S_PIECES[n]
                            nc.scalar.copy(scores[:, u % SLOTS, t, lo:hi], at[:, 0:hi - lo]).then_inc(piece_used, 1)
                        else:
                            rows = P if T_PIECES[n][-1] < KCHUNKS - 1 else LAST_KEYS
                            w = len(T_PIECES[n]) * BANK
                            nc.scalar.activation(attn[0:rows, n, 0:w], at[0:rows, 0:w], ACT.Relu).then_inc(piece_used, 1)
                    if g == 0 and has(i, LAG + 1):
                        act.wait_ge(products, NT * (i - LAG))
                        if not isinstance(i, int) or i > LAG + 1:
                            act.wait_ge(out_stored, 64 * (i - LAG - 1))
                        nc.scalar.copy(o_sb[:], out_ps[:]).then_inc(out_copied, 1)
                    if g == 0 and has(i, 2):
                        measure_excess(i - 2, (u - 2) % SLOTS, ROUNDS - 1)
                    if g > 0 and has(i, 1):
                        measure_excess(i - 1, (u - 1) % SLOTS, g - 1)

            walk(act, step)

        @block.vector
        def _(dve):
            nc.vector.memset(k_st[SCORE_ROWS:SCORE_ROWS + TAU_ROWS], 1.0).then_inc(setup, 1)
            nc.vector.memset(ones[:], 1.0).then_inc(setup, 1)
            nc.vector.memset(zeros[:], 0.0).then_inc(setup, 1)
            nc.vector.memset(out_ps[:], 0.0).then_inc(setup, 1)
            nc.vector.memset(flag[:], 0.0).then_inc(chain, 1)
            dve.wait_ge(ident_loaded, 16)
            nc.vector.tensor_copy(ident[:], ident_f[:]).then_inc(setup, 1)
            dve.wait_ge(setup, SETUP)
            dve.wait_ge(chain, 1)
            unsettled = [dve.alloc_register(f"unsettled{t}") for t in range(TILES)]
            all_bad = dve.alloc_register("all_bad")
            steps_left = dve.alloc_register("steps_left")
            quadrant = [dve.alloc_register(f"quadrant{t}") for t in range(4)]

            def measure_own(t, values, width):
                return nc.vector.scalar_tensor_tensor(out=view(junk, values, width, TILES + t), in0=values, scalar=tau[:, t:t + 1], in1=zeros_like(values), op0=ALU.subtract, op1=ALU.max,
                                                      accum_out=own_excess[:, t:t + 1])

            def measure_count(t, values, width):
                return nc.vector.tensor_scalar(view(junk, values, width, t), values, tau[:, t:t + 1], None, ALU.is_gt, ALU.add, accum_out=count[:, t:t + 1])

            def view(tile, values, width, n):
                flat = tile[:, n * width:(n + 1) * width]
                return flat.rearrange("p (a b) -> p a b", a=CHUNKS) if len(values.shape) == 3 else flat

            def zeros_like(values):
                return (zeros[:].unsqueeze(2) if len(values.shape) == 3 else zeros[:]).broadcast_to(list(values.shape))

            V = nc.vector


            def guess(link, excess_in):
                yield from link(V.tensor_scalar(count[:], count[:], 1.0, None, ALU.max))
                yield from link(V.scalar_tensor_tensor(out=w1[:], in0=excess_in, scalar=1.0, in1=count[:], op0=ALU.add, op1=ALU.mult))
                yield from link(V.reciprocal(inv[:], w1[:]))
                yield from link(V.scalar_tensor_tensor(out=w2[:], in0=excess_in, scalar=1.0, in1=excess_in, op0=ALU.subtract, op1=ALU.mult))
                yield from link(V.scalar_tensor_tensor(out=move[:], in0=w2[:], scalar=2.0, in1=inv[:], op0=ALU.mult, op1=ALU.mult))
                yield from link(V.tensor_tensor(tau[:], tau[:], move[:], ALU.add))

            def start(link, c):
                yield from link(V.tensor_reduce(top[:], c[:, :, :, 0], AX.X, ALU.max))
                yield from link(V.tensor_reduce(w1[:], c[:, :, :, 0], AX.X, ALU.add))
                yield from link(V.tensor_scalar(tau[:], w1[:], 1.0 / CHUNKS, None, ALU.mult))
                for t in range(TILES):
                    measure_own(t, c[:, t, :, 0:FIRST], CHUNKS * FIRST)
                    ins = measure_count(t, c[:, t, :, 0:FIRST], CHUNKS * FIRST)
                yield from link(ins)
                yield from guess(link, own_excess[:])
                V.tensor_scalar(ntau[:], tau[:], -1.0, None, ALU.mult).then_inc(tau_tried, 1)
                for t in range(TILES):
                    ins = measure_count(t, c[:, t, :, 0:SECOND], CHUNKS * SECOND)
                yield from link(ins)

            def second(i, link, c):
                dve.wait_ge(excess_made, ROUNDS * i + 1)
                yield from guess(link, excess[:])
                yield from link(V.scalar_tensor_tensor(out=tau[:], in0=top[:], scalar=1.0, in1=tau[:], op0=ALU.subtract, op1=ALU.max))
                yield from link(V.scalar_tensor_tensor(out=tau[:], in0=top[:], scalar=1.0 / KEYS, in1=tau[:], op0=ALU.subtract, op1=ALU.min))
                V.tensor_scalar(ntau[:], tau[:], -1.0, None, ALU.mult).then_inc(tau_tried, 1)
                for t in range(TILES):
                    ins = measure_count(t, c[:, t].rearrange("p a b -> p (a b)"), CAND)
                yield from link(ins)
                yield from link(V.tensor_scalar(count[:], count[:], 1.0, None, ALU.max))
                yield from link(V.reciprocal(inv[:], count[:]))

            def newton(i, link, r):
                dve.wait_ge(excess_made, ROUNDS * i + r + 1)
                yield from link(V.scalar_tensor_tensor(out=move[:], in0=excess[:], scalar=1.0, in1=inv[:], op0=ALU.subtract, op1=ALU.mult))
                yield from link(V.tensor_tensor(tau[:], tau[:], move[:], ALU.add))
                if r < ROUNDS - 1:
                    V.tensor_scalar(ntau[:], tau[:], -1.0, None, ALU.mult).then_inc(tau_tried, 1)

            def judge(link, c):
                yield from link(V.tensor_scalar(w1[:], excess[:], 1.0, None, ALU.subtract))
                yield from link(V.tensor_tensor(w1[:], w1[:], w1[:], ALU.mult))
                yield from link(V.tensor_reduce(w2[:], c[:, :, :, 7], AX.X, ALU.max))
                yield from link(V.tensor_tensor(w2[:], w2[:], tau[:], ALU.is_gt))
                yield from link(V.tensor_copy(found[:], tau[:]))
                V.scalar_tensor_tensor(out=bad[:], in0=w1[:], scalar=EXACT ** 2, in1=w2[:], op0=ALU.is_gt, op1=ALU.max).then_inc(bad_ready, 1)

            FIRST_LINKS = (4 + 6 + 1) + (6 + 2 + 1 + 2) + (ROUNDS - 2) * 2
            LAST_LINKS = 2 + 5 + 5

            def links_before(i):
                if isinstance(i, int):
                    return 1 + FIRST_LINKS * min(max(0, i - 1), N) + LAST_LINKS * min(max(0, i - 2), N)
                return i * (FIRST_LINKS + LAST_LINKS) + (1 - FIRST_LINKS - 2 * LAST_LINKS)

            def general_path(t, sc):
                dve.sem_clear(general)
                links = [0]

                def link(ins):
                    links[0] += 1
                    ins.then_inc(general, 1)
                    dve.wait_ge(general, links[0])

                c = slice(t, t + 1)
                link(V.scalar_tensor_tensor(out=junk[:], in0=sc, scalar=found[:, c], in1=zeros[:].broadcast_to([P, KEYS]), op0=ALU.subtract, op1=ALU.max,
                                            accum_out=g_excess[:, c]))
                link(V.tensor_scalar(junk[:], sc, found[:, c], None, ALU.is_gt, ALU.add, accum_out=g_count[:, c]))
                link(V.tensor_scalar(g_count[:, c], g_count[:, c], 1.0, None, ALU.max))
                link(V.reciprocal(g_count[:, c], g_count[:, c]))
                link(V.scalar_tensor_tensor(out=g1[:, c], in0=g_excess[:, c], scalar=1.0, in1=g_count[:, c], op0=ALU.subtract, op1=ALU.mult))
                link(V.tensor_tensor(found[:, c], found[:, c], g1[:, c], ALU.add))
                link(V.tensor_tensor(g1[:, c], g1[:, c], g1[:, c], ALU.mult))
                link(V.tensor_tensor(g2[:, c], found[:, c], found[:, c], ALU.mult))
                link(V.tensor_scalar(g2[:, c], g2[:, c], SETTLED ** 2, SETTLED ** 2, ALU.mult, ALU.add))
                link(V.tensor_tensor(flag[:, 0:1], g1[:, c], g2[:, c], ALU.is_gt))
                link(V.transpose(flag_t[:], flag[:]))
                with nc.allow_low_precision(reason="counts up to 32 are exact as integers"):
                    link(V.tensor_reduce(flag_i[:], flag_t[:], AX.X, ALU.add))
                for q in range(4):
                    dve.reg_load(quadrant[q], flag_i[32 * q:32 * q + 1, 0:1])
                dve.reg_add(quadrant[0], quadrant[0], quadrant[1])
                dve.reg_add(quadrant[2], quadrant[2], quadrant[3])
                dve.reg_add(quadrant[0], quadrant[0], quadrant[2])
                dve.reg_sub(steps_left, steps_left, 1)
                dve.reg_mul(unsettled[t], quadrant[0], steps_left)

            def settle(i, u, link):
                dve.wait_ge(bad_counted, i + 1)
                yield from link(V.tensor_copy(bad_i[:], turn_ps[0:1, 0:TILES + 1]))
                dve.sem_inc(passed, 1)
                dve.reg_load(all_bad, bad_i[0:1, TILES:TILES + 1])
                with dve.If(dve.snap(all_bad) > 0):
                    for t in range(TILES):
                        dve.reg_load(unsettled[t], bad_i[0:1, t:t + 1])
                    for t in range(TILES):
                        with dve.If(dve.snap(unsettled[t]) > 0):
                            dve.reg_mov(steps_left, GENERAL_STEPS)
                            with dve.While(lambda: dve.snap(unsettled[t]) > 0):
                                general_path(t, scores[:, u, t])
                yield from link(V.tensor_scalar(neg[:], found[:], -1.0, None, ALU.mult))
                yield from link(V.tensor_copy(split[:, :, 0], neg[:]))
                yield from link(V.tensor_tensor(neg[:], neg[:], split[:, :, 0], ALU.subtract))
                yield from link(V.tensor_copy(split[:, :, 1], neg[:]))
                V.tensor_tensor(split[:, :, 2], neg[:], split[:, :, 1], ALU.subtract).then_inc(tau_split, 1)

            def step(i, u):
                made = [links_before(i)]

                def link(ins):
                    made[0] = made[0] + 1
                    ins.then_inc(chain, 1)
                    own = made[0]
                    yield
                    dve.wait_ge(chain, own)

                def beside(t):
                    if t == 0 and has(i, 2):
                        yield from newton(i - 2, link, ROUNDS - 1)
                        yield from judge(link, cand[:, (u - 2) % SLOTS])
                    if t == 0 and has(i, 1):
                        dve.wait_ge(cand_made, i)
                        yield from start(link, cand[:, (u - 1) % SLOTS])
                    if t == 1 and has(i, 1):
                        yield from second(i - 1, link, cand[:, (u - 1) % SLOTS])
                    if t > 1 and has(i, 1):
                        yield from newton(i - 1, link, t - 1)
                    if t == 2 and has(i, 2):
                        yield from settle(i - 2, (u - 2) % SLOTS, link)
                    dve.sem_inc(passed, 1)

                for t in range(TILES):
                    side = beside(t)
                    if has(i, 0):
                        dve.wait_ge(piece_used, before(i) + score_place(2 * t + 1, has(i, LAG)) + 1)
                        dve.sem_inc(passed, 1)
                        for c, (lo, hi) in enumerate(RUNS):
                            ins = V.max(cand[:, u % SLOTS, t, c], scores[:, u % SLOTS, t, lo:hi])
                            if c % 2:
                                next(side, None)
                        if t == TILES - 1:
                            ins.then_inc(cand_made, 1)
                    for _ in side:
                        pass

            walk(dve, step)


def experts_program(nc, x, g_attn, g_ffn, wo, bo, o_parts, router_w, w_in, b_in, w_out, b_out, ident_in, out):
    with ExitStack() as ctx:
        def sb(name, shape, dt=F32):
            return ctx.enter_context(nc.sbuf_tensor("e_" + name, shape, dt))

        def sem(name):
            return ctx.enter_context(nc.semaphore("e_" + name))

        def ps(name, banks):
            return ctx.enter_context(nc.psum_tensor("e_" + name, [P, banks, BANK], F32))

        hid_ps = ps("hid_ps", 4)
        y_ps = ps("y_ps", 2)
        turn_ps = ps("turn_ps", 2)
        y_tile = [y_ps[:, t // 2, (t % 2) * DIM:(t % 2 + 1) * DIM] for t in range(TILES)]

        win_s = sb("w_in", [P, EXPERTS, HALVES, HIDDEN])
        wout_s = sb("w_out", [P, EXPERTS, HALVES, DIM])
        bin_s = sb("b_in", [P, EXPERTS, HALVES])
        bout_s = sb("b_out", [EXPERTS, DIM])
        wo_s = sb("wo", [P, HALVES, DIM])
        wr_s = sb("router", [P, HALVES, EXPERTS])
        bo_s = sb("bo", [P, DIM])
        ident = sb("ident", [P, P])
        g_s = sb("g", [P, 2])
        gates = sb("gates", [P, 2])
        places = sb("places", [P, EXPERTS])
        places_i = sb("places_i", [P, EXPERTS], I32)
        x_s = sb("x", [P, TILES, DIM])
        o_s = sb("o", [P, HALVES, 4, QUERIES])
        osum = sb("osum", [P, HALVES, QUERIES])
        x2 = sb("x2", [P, TILES, DIM])
        stats = sb("stats", [P, TILES, 6])
        moments = sb("moments", [P, TILES, 2])
        veps, std, rstd, fix = (sb(n, [P, TILES]) for n in ("veps", "std", "rstd", "fix"))
        xn = sb("xn", [P, TILES, DIM])
        xnt = sb("xnt", [P, HALVES, QUERIES])
        logits = sb("logits", [P, TILES, EXPERTS])
        best = sb("best", [P, TILES, 8])
        best_i = sb("best_i", [P, TILES, 8], U32)
        best_f = sb("best_f", [P, TILES, 8])
        nbest = sb("nbest", [P, TILES])
        prob = sb("prob", [P, TILES, EXPERTS])
        mass = sb("mass", [P, TILES])
        rmass = sb("rmass", [P, TILES])
        pick = sb("pick", [P, TILES, EXPERTS])
        pick2 = sb("pick2", [P, TILES, EXPERTS])
        gate = sb("gate", [P, TILES, EXPERTS])
        gate_t = sb("gate_t", [EXPERTS, QUERIES])
        hid = sb("hid", [P, 2, HALVES, QUERIES])
        acc = sb("acc", [P, TILES, DIM])
        res = sb("res", [P, TILES, DIM])

        weights, x_loaded, o_loaded, stored = sem("weights"), sem("x_loaded"), sem("o_loaded"), sem("stored")
        g_tanh = sem("g_tanh")
        places_made = sem("places_made")
        consts = sem("consts")
        chain = sem("chain")
        o_summed = sem("o_summed")
        projected = sem("projected")
        x2_done = sem("x2_done")
        stats_done = sem("stats_done")
        std_done = sem("std_done")
        normed = sem("normed")
        turned = sem("turned")
        xnt_done = sem("xnt_done")
        routed = sem("routed")
        best_done = sem("best_done")
        exp_done = sem("exp_done")
        gate_done = sem("gate_done")
        gate_turned = sem("gate_turned")
        gate_t_done = sem("gate_t_done")
        bias_made = sem("bias_made")
        hid_made = sem("hid_made")
        hid_done = sem("hid_done")
        y_made = sem("y_made")
        passed = sem("passed")
        y_used = sem("y_used")
        finished = sem("finished")
        LOADS = 9 + EXPERTS * HALVES

        block = ctx.enter_context(nc.Block())

        @block.sync
        def _(sp):
            sp.dma_start(win_s[:], w_in.rearrange("e (a p) n -> p e a n", p=P)).then_inc(weights, 16)
            sp.dma_start(wout_s[:], w_out.rearrange("e (a p) n -> p e a n", p=P)).then_inc(weights, 16)
            for e in range(EXPERTS):
                for a in range(HALVES):
                    sp.dma_start(bin_s[:, e, a:a + 1], b_in[e, a * P:(a + 1) * P].rearrange("(p o) -> p o", o=1)).then_inc(weights, 16)
            sp.dma_start(bout_s[:], b_out).then_inc(weights, 16)
            sp.dma_start(wo_s[:], wo.rearrange("(a p) n -> p a n", p=P)).then_inc(weights, 16)
            sp.dma_start(wr_s[:], router_w.rearrange("(a p) n -> p a n", p=P)).then_inc(weights, 16)
            sp.dma_start(bo_s[:], bo.rearrange("(o n) -> o n", o=1).broadcast_to([P, DIM])).then_inc(weights, 16)
            sp.dma_start(ident[:], ident_in).then_inc(weights, 16)
            for n, g in enumerate((g_attn, g_ffn)):
                sp.dma_start(g_s[:, n:n + 1], g.rearrange("(o n) -> o n", o=1).broadcast_to([P, 1])).then_inc(weights, 16)
            with sp.Fori(0, BATCH) as b:
                sp.wait_ge(x2_done, TILES * b)
                sp.dma_start(x_s[:], x[b].rearrange("(t p) d -> p t d", p=P)).then_inc(x_loaded, 16)
                for s in range(4):
                    sp.dma_start(o_s[:, :, s], o_parts[s, bass.ds(b * DIM, DIM)].rearrange("(a p) n -> p a n", p=P)).then_inc(o_loaded, 16)

        @block.gpsimd
        def _(pool):
            nc.gpsimd.iota(places_i[:], pattern=[[1, EXPERTS]], base=0, channel_multiplier=0).then_inc(places_made, 1)
            with pool.Fori(0, BATCH) as b:
                pool.wait_ge(finished, TILES * (b + 1))
                pool.dma_start(out[b].rearrange("(t p) d -> p t d", p=P), res[:]).then_inc(stored, 16)
            pool.wait_ge(stored, 16 * BATCH)

        @block.tensor
        def _(pe):
            pe.wait_ge(weights, 16 * LOADS)
            with pe.Fori(0, BATCH) as b:
                pe.wait_ge(o_summed, b + 1)
                pe.wait_ge(y_used, (EXPERTS + 1) * b)
                for t in range(TILES):
                    for a in range(HALVES):
                        mm = nc.tensor.matmul(y_tile[t], osum[:, a, t * P:(t + 1) * P], wo_s[:, a], start=a == 0, stop=a == HALVES - 1, skip_group_check=True)
                mm.then_inc(projected, 1)
                pe.wait_ge(normed, TILES * (b + 1))
                for a in range(HALVES):
                    for t in range(TILES):
                        mm = nc.tensor.transpose(turn_ps[:, a, t * P:(t + 1) * P], xn[:, t, a * P:(a + 1) * P], ident[:])
                mm.then_inc(turned, 1)
                pe.wait_ge(xnt_done, HALVES * (b + 1))
                for t in range(TILES):
                    for a in range(HALVES):
                        mm = nc.tensor.matmul(turn_ps[:, 0, t * EXPERTS:(t + 1) * EXPERTS], xnt[:, a, t * P:(t + 1) * P], wr_s[:, a], start=a == 0, stop=a == HALVES - 1, skip_group_check=True)
                mm.then_inc(routed, 1)

                def hidden(e):
                    for m in range(HALVES):
                        n = e * HALVES + m
                        pe.wait_ge(hid_done, HALVES * EXPERTS * b + n - 2 * HALVES + 1) if n >= 2 * HALVES else pe.wait_ge(hid_done, HALVES * EXPERTS * b)
                        for a in range(HALVES):
                            mm = nc.tensor.matmul(hid_ps[:, n % 4], win_s[:, e, a, m * P:(m + 1) * P], xnt[:, a], start=a == 0, stop=a == HALVES - 1)
                        mm.then_inc(hid_made, 1)

                hidden(0)
                pe.wait_ge(gate_done, b + 1)
                for t in range(TILES):
                    mm = nc.tensor.transpose(turn_ps[0:EXPERTS, 1, t * P:(t + 1) * P], gate[:, t], ident[:])
                mm.then_inc(gate_turned, 1)
                hidden(1)
                pe.wait_ge(gate_t_done, b + 1)
                for t in range(TILES):
                    mm = nc.tensor.matmul(y_tile[t], gate_t[:, t * P:(t + 1) * P], bout_s[:], start=True, stop=True, skip_group_check=True)
                mm.then_inc(bias_made, 1)
                for e in range(EXPERTS):
                    pe.wait_ge(hid_done, HALVES * (EXPERTS * b + e + 1))
                    pe.wait_ge(y_used, (EXPERTS + 1) * b + e + 1)
                    for t in range(TILES):
                        for a in range(HALVES):
                            mm = nc.tensor.matmul(y_tile[t], hid[:, e % 2, a, t * P:(t + 1) * P], wout_s[:, e, a], start=a == 0, stop=a == HALVES - 1, skip_group_check=True)
                    mm.then_inc(y_made, 1)
                    if e + 2 < EXPERTS:
                        hidden(e + 2)

        @block.scalar
        def _(act):
            act.wait_ge(weights, 16 * LOADS)
            nc.scalar.activation(gates[:], g_s[:], ACT.Tanh).then_inc(g_tanh, 1)
            with act.Fori(0, BATCH) as b:
                act.wait_ge(stats_done, b + 1)
                nc.scalar.activation(std[:], veps[:], ACT.Sqrt).then_inc(std_done, 1)
                act.wait_ge(best_done, b + 1)
                for t in range(TILES):
                    ins = nc.scalar.activation(prob[:, t], logits[:, t], ACT.Exp, bias=nbest[:, t:t + 1], accum_out=mass[:, t:t + 1])
                ins.then_inc(exp_done, 1)
                for e in range(EXPERTS):
                    for m in range(HALVES):
                        n = e * HALVES + m
                        act.wait_ge(hid_made, HALVES * EXPERTS * b + n + 1)
                        if m == 0:
                            if e >= 2:
                                act.wait_ge(y_made, EXPERTS * b + e - 1)
                            else:
                                act.wait_ge(y_made, EXPERTS * b)
                        nc.scalar.activation(hid[:, e % 2, m], hid_ps[:, n % 4], ACT.Gelu_apprx_tanh, bias=bin_s[:, e, m:m + 1]).then_inc(hid_done, 1)

        @block.vector
        def _(dve):
            V = nc.vector
            dve.wait_ge(weights, 16 * LOADS)
            dve.wait_ge(g_tanh, 1)
            dve.wait_ge(places_made, 1)
            V.tensor_copy(places[:], places_i[:]).then_inc(consts, 1)
            V.tensor_scalar(bo_s[:], bo_s[:], gates[:, 0:1], None, ALU.mult).then_inc(consts, 1)
            dve.wait_ge(consts, 2)
            LINKS = 2 + 1 + 2 + 5 + 1 + 2 + 6

            with dve.Fori(0, BATCH) as b:
                made = [b * LINKS]

                def link(ins):
                    made[0] = made[0] + 1
                    ins.then_inc(chain, 1)
                    dve.wait_ge(chain, made[0])

                dve.wait_ge(o_loaded, 64 * (b + 1))
                link(V.tensor_tensor(osum[:], o_s[:, :, 0], o_s[:, :, 1], ALU.add))
                link(V.tensor_tensor(osum[:], osum[:], o_s[:, :, 2], ALU.add))
                V.tensor_tensor(osum[:], osum[:], o_s[:, :, 3], ALU.add).then_inc(o_summed, 1)
                dve.wait_ge(x_loaded, 16 * (b + 1))
                for t in range(TILES):
                    ins = V.tensor_tensor(x2[:, t], x_s[:, t], bo_s[:], ALU.add)
                link(ins)
                dve.wait_ge(projected, b + 1)
                for t in range(TILES):
                    V.scalar_tensor_tensor(out=x2[:, t], in0=y_tile[t], scalar=gates[:, 0:1], in1=x2[:, t], op0=ALU.mult, op1=ALU.add).then_inc(x2_done, 1)
                dve.wait_ge(x2_done, TILES * (b + 1))
                for t in range(TILES):
                    ins = V.bn_stats(stats[:, t], x2[:, t])
                link(ins)
                dve.sem_inc(passed, 1)
                for t in range(TILES):
                    ins = V.bn_aggr(moments[:, t], stats[:, t])
                link(ins)
                V.tensor_scalar(veps[:], moments[:, :, 1], EPS, None, ALU.add).then_inc(stats_done, 1)
                dve.wait_ge(std_done, b + 1)
                link(V.reciprocal(rstd[:], std[:]))
                link(V.tensor_tensor(fix[:], rstd[:], rstd[:], ALU.mult))
                link(V.tensor_tensor(fix[:], fix[:], veps[:], ALU.mult))
                link(V.tensor_scalar(fix[:], fix[:], -0.5, 1.5, ALU.mult, ALU.add))
                link(V.tensor_tensor(rstd[:], rstd[:], fix[:], ALU.mult))
                for t in range(TILES):
                    V.tensor_scalar(xn[:, t], x2[:, t], moments[:, t, 0:1], rstd[:, t:t + 1], ALU.subtract, ALU.mult).then_inc(normed, 1)
                dve.wait_ge(turned, b + 1)
                for a in range(HALVES):
                    V.tensor_copy(xnt[:, a], turn_ps[:, a]).then_inc(xnt_done, 1)
                dve.wait_ge(routed, b + 1)
                link(V.tensor_copy(logits[:], turn_ps[:, 0, 0:TILES * EXPERTS].rearrange("p (t e) -> p t e", t=TILES)))
                dve.sem_inc(passed, 1)
                for t in range(TILES):
                    ins = V.max(best[:, t], logits[:, t])
                link(ins)
                dve.sem_inc(passed, 1)
                for t in range(TILES):
                    ins = V.max_index(best_i[:, t], best[:, t], logits[:, t])
                link(ins)
                V.tensor_scalar(nbest[:], best[:, :, 0], -1.0, None, ALU.mult).then_inc(best_done, 1)
                link(V.tensor_copy(best_f[:], best_i[:]))
                every = places[:].unsqueeze(1).broadcast_to([P, TILES, EXPERTS])
                link(V.tensor_tensor(pick[:], every, best_f[:, :, 0:1].broadcast_to([P, TILES, EXPERTS]), ALU.is_equal))
                link(V.tensor_tensor(pick2[:], every, best_f[:, :, 1:2].broadcast_to([P, TILES, EXPERTS]), ALU.is_equal))
                link(V.tensor_tensor(pick[:], pick[:], pick2[:], ALU.add))
                dve.wait_ge(exp_done, b + 1)
                link(V.reciprocal(rmass[:], mass[:]))
                link(V.tensor_tensor(pick[:], pick[:], prob[:], ALU.mult))
                V.tensor_tensor(gate[:], pick[:], rmass[:].unsqueeze(2).broadcast_to([P, TILES, EXPERTS]), ALU.mult).then_inc(gate_done, 1)
                dve.wait_ge(gate_turned, b + 1)
                V.tensor_copy(gate_t[:], turn_ps[0:EXPERTS, 1]).then_inc(gate_t_done, 1)
                dve.wait_ge(bias_made, b + 1)
                for t in range(TILES):
                    ins = V.tensor_copy(acc[:, t], y_tile[t])
                ins.then_inc(y_used, 1)
                for e in range(EXPERTS):
                    dve.wait_ge(y_made, EXPERTS * b + e + 1)
                    dve.wait_ge(y_used, (EXPERTS + 1) * b + e + 1)
                    for t in range(TILES):
                        ins = V.scalar_tensor_tensor(out=acc[:, t], in0=y_tile[t], scalar=gate[:, t, e:e + 1], in1=acc[:, t], op0=ALU.mult, op1=ALU.add)
                    ins.then_inc(y_used, 1)
                dve.wait_ge(y_used, (EXPERTS + 1) * (b + 1))
                dve.wait_ge(stored, 16 * b)
                for t in range(TILES):
                    V.scalar_tensor_tensor(out=res[:, t], in0=acc[:, t], scalar=gates[:, 1:2], in1=x2[:, t], op0=ALU.mult, op1=ALU.add).then_inc(finished, 1)


def program(nc, x, ctx_t, ident, g_xattn, g_ffn, wq, bq, wk, bk, wv, bv, wo, bo, router_w, w_in, b_in, w_out, b_out, out):
    q_parts = nc.dram_tensor("q_parts", (3, BATCH * DIM, QUERIES), BF16).ap()
    k_parts = nc.dram_tensor("k_parts", (3, BATCH * DIM, KEYS), BF16).ap()
    v_heads = nc.dram_tensor("v_heads", (BATCH * HEADS, P, KCHUNKS, HEAD_DIM), F32).ap()
    o_parts = nc.dram_tensor("o_parts", (4, BATCH * DIM, QUERIES), F32).ap()
    project_program(nc, x, ctx_t, wq, bq, wk, bk, wv, bv, ident, q_parts, k_parts, v_heads)
    attend_program(nc, q_parts, k_parts, v_heads, ident, o_parts)
    experts_program(nc, x, g_xattn, g_ffn, wo, bo, o_parts, router_w, w_in, b_in, w_out, b_out, ident, out)


_INS = ["x", "ctx_t", "ident", "g_xattn", "g_ffn", "L0_xattn_Wq", "L0_xattn_bq", "L0_xattn_Wk", "L0_xattn_bk",
        "L0_xattn_Wv", "L0_xattn_bv", "L0_xattn_Wo", "L0_xattn_bo", "L0_ffn_router_w", "L0_ffn_w_in", "L0_ffn_b_in",
        "L0_ffn_w_out", "L0_ffn_b_out"]


def kernel(**inputs):
    import numpy as np
    import concourse.bacc as bacc
    from concourse.bass_utils import run_bass_kernel_spmd

    nc = bacc.Bacc("TRN2", target_bir_lowering=False, num_devices=1)
    laid = dict(inputs)
    laid["ctx_t"] = np.transpose(np.asarray(inputs["ctx_1024"]), (0, 2, 1))
    laid["ident"] = np.eye(P, dtype=np.float32)
    arrays, args = {}, []
    for name in _INS:
        a = np.ascontiguousarray(laid[name])
        arrays[f"in_{name}"] = a
        args.append(nc.dram_tensor(f"in_{name}", a.shape, mybir.dt.from_np(a.dtype), kind="ExternalInput").ap())
    out = nc.dram_tensor("out_0", (BATCH, QUERIES, DIM), F32, kind="ExternalOutput").ap()
    program(nc, *args, out)
    r = run_bass_kernel_spmd(nc, [arrays], core_ids=[0])
    return r.results[0]["out_0"]
```

```python
from contextlib import ExitStack

import concourse.bass as bass
from concourse import mybir

F32 = mybir.dt.float32
BF16 = mybir.dt.bfloat16
I32 = mybir.dt.int32
U32 = mybir.dt.uint32
ALU = mybir.AluOpType
ACT = mybir.ActivationFunctionType
AX = mybir.AxisListType

P = 128
BATCH, QUERIES, KEYS, DIM = 16, 512, 1601, 256
HEADS, HEAD_DIM = 16, 16
EXPERTS, HIDDEN = 8, 256
SCALE = HEAD_DIM ** -0.5
EPS = 1e-5
HALVES = DIM // P
TILES = QUERIES // P
KCHUNKS = -(-KEYS // P)
LAST_KEYS = KEYS - (KCHUNKS - 1) * P
BANK = 512
KEY_PIECES = [(c, min(c + BANK, KEYS)) for c in range(0, KEYS, BANK)]

K_PARTS = [0, 1, 2, 0, 1, 0]
Q_PARTS = [0, 0, 0, 1, 1, 2]
GROUPS = len(K_PARTS)
SCORE_ROWS = GROUPS * HEAD_DIM
TAU_ROWS = 3

CHUNKS = 36
RUNS = [(KEYS * c // CHUNKS, KEYS * (c + 1) // CHUNKS) for c in range(CHUNKS)]
CAND = CHUNKS * 8
FIRST, SECOND = 2, 4
ROUNDS = 5
EXACT = 3e-5
GENERAL_STEPS = 26


def project_program(nc, x, ctx_t, wq, bq, wk, bk, wv, bv, ident_in, q_parts, k_parts, v_heads):
    with ExitStack() as ctx:
        def sb(name, shape, dt=F32):
            return ctx.enter_context(nc.sbuf_tensor("p_" + name, shape, dt))

        def sem(name):
            return ctx.enter_context(nc.semaphore("p_" + name))

        RING = 5
        ring = ctx.enter_context(nc.psum_tensor("p_ring", [P, RING, BANK], F32))
        xt = sb("x", [P, 2, TILES, DIM])
        ct = sb("ctx", [P, 2, HALVES, KEYS])
        wq_s, wk_s, wv_s = (sb(n, [P, HALVES, DIM]) for n in ("wq", "wk", "wv"))
        bq_s, bk_s = sb("bq", [P, HALVES]), sb("bk", [P, HALVES])
        bqs = sb("bqs", [P, HALVES])
        bv_s = sb("bv", [P, DIM])
        ident = sb("ident", [P, P])
        stats = sb("stats", [P, TILES, 6])
        moments = sb("moments", [P, TILES, 2])
        std = sb("std", [P, TILES])
        veps = sb("veps", [P, TILES])
        rstd = sb("rstd", [P, TILES])
        fix = sb("fix", [P, TILES])
        xn = sb("xn", [P, TILES, DIM])
        xnt = sb("xnt", [P, HALVES, QUERIES])
        qf = sb("qf", [P, HALVES, QUERIES])
        qr = sb("qr", [P, HALVES, QUERIES])
        qs = sb("qs", [P, 3, HALVES, QUERIES], BF16)
        kf = sb("kf", [P, HALVES, KEYS])
        kr = sb("kr", [P, HALVES, KEYS])
        ks = sb("ks", [P, 3, HALVES, KEYS], BF16)
        vt = sb("v", [P, HEADS, KCHUNKS, HEAD_DIM])

        weights = sem("weights")
        x_loaded = [sem("x_loaded0"), sem("x_loaded1")]
        ctx_loaded = [sem("ctx_loaded0"), sem("ctx_loaded1")]
        stats_done = sem("stats_done")
        std_done = sem("std_done")
        chain = sem("chain")
        normed = sem("normed")
        job_made = sem("job_made")
        job_used = sem("job_used")
        job_used_dve = sem("job_used_dve")
        passed, passed_sp = sem("passed"), sem("passed_sp")
        q_rest = sem("q_rest")
        k_rest = sem("k_rest")
        q_split = sem("q_split")
        k_split = sem("k_split")
        q_high = sem("q_high")
        k_high = sem("k_high")
        q_mid = sem("q_mid")
        k_mid = sem("k_mid")
        q_stored = sem("q_stored")
        k_stored = sem("k_stored")
        v_stored = sem("v_stored")
        consts = sem("consts")

        jobs = [("turn", a) for a in range(HALVES)]
        jobs += [("k", a, c) for a in range(HALVES) for c in range(len(KEY_PIECES))]
        jobs += [("q", a) for a in range(HALVES)]
        jobs += [("v", c) for c in range(KCHUNKS)]
        NJ = len(jobs)
        assert NJ % RING == 0
        by_dve = [j[0] in ("turn", "v") for j in jobs]
        dve_jobs, act_jobs = sum(by_dve), NJ - sum(by_dve)

        def readers_before(b, n):
            return b * dve_jobs + sum(by_dve[:n]), b * act_jobs + n - sum(by_dve[:n])

        block = ctx.enter_context(nc.Block())

        @block.sync
        def _(sp):
            for dst, src in ((wq_s, wq), (wk_s, wk), (wv_s, wv)):
                sp.dma_start(dst[:], src.rearrange("(a p) n -> p a n", p=P)).then_inc(weights, 16)
            for dst, src in ((bq_s, bq), (bk_s, bk)):
                for a in range(HALVES):
                    sp.dma_start(dst[:, a:a + 1], src[a * P:(a + 1) * P].rearrange("(p o) -> p o", o=1)).then_inc(weights, 16)
            sp.dma_start(bv_s[:], bv.rearrange("(o n) -> o n", o=1).broadcast_to([P, DIM])).then_inc(weights, 16)
            sp.dma_start(ident[:], ident_in).then_inc(weights, 16)

            def load(b, u, first):
                if not first:
                    sp.wait_ge(normed, TILES * (b - 1))
                    sp.sem_inc(passed_sp, 1)
                    sp.wait_ge(job_made, NJ * (b - 1))
                    sp.sem_inc(passed_sp, 1)
                sp.dma_start(xt[:, u], x[b].rearrange("(t p) d -> p t d", p=P)).then_inc(x_loaded[u], 16)
                sp.dma_start(ct[:, u], ctx_t[b].rearrange("(a p) n -> p a n", p=P)).then_inc(ctx_loaded[u], 16)

            def store(b):
                sp.wait_ge(q_split, b + 1)
                for s in range(3):
                    sp.dma_start(q_parts[s, bass.ds(b * DIM, DIM)].rearrange("(a p) n -> p a n", p=P), qs[:, s]).then_inc(q_stored, 16)
                sp.wait_ge(k_split, b + 1)
                for s in range(3):
                    sp.dma_start(k_parts[s, bass.ds(b * DIM, DIM)].rearrange("(a p) n -> p a n", p=P), ks[:, s]).then_inc(k_stored, 16)
                sp.wait_ge(job_used_dve, dve_jobs * (b + 1))
                sp.dma_start(v_heads[bass.ds(b * HEADS, HEADS)].rearrange("h p c d -> p h c d")[:, :, 0:KCHUNKS - 1], vt[:, :, 0:KCHUNKS - 1]).then_inc(v_stored, 16)
                sp.dma_start(v_heads[bass.ds(b * HEADS, HEADS)].rearrange("h p c d -> p h c d")[0:LAST_KEYS, :, KCHUNKS - 1:], vt[0:LAST_KEYS, :, KCHUNKS - 1:]).then_inc(v_stored, 16)

            load(0, 0, True)
            load(1, 1, True)
            if BATCH > 2:
                with sp.Fori(0, BATCH // 2 - 1) as g:
                    for u in range(2):
                        store(2 * g + u)
                        load(2 * g + u + 2, u, False)
            for b in range(BATCH - 2, BATCH):
                store(b)
            sp.wait_ge(q_stored, 16 * 3 * BATCH)
            sp.wait_ge(k_stored, 16 * 3 * BATCH)
            sp.wait_ge(v_stored, 16 * 2 * BATCH)

        @block.tensor
        def _(pe):
            pe.wait_ge(weights, 16 * 9)
            def pair(g):
                for u in range(2):
                    b = 2 * g + u
                    pe.wait_ge(normed, TILES * (b + 1))
                    for n, job in enumerate(jobs):
                        bank = ring[:, n % RING]
                        if n >= RING:
                            by, m = by_dve[n - RING], n - RING
                            d, a = readers_before(b, m + 1)
                            pe.wait_ge(job_used_dve if by else job_used, d if by else a)
                        elif not isinstance(b, int) or b > 0:
                            m = NJ + n - RING
                            by = by_dve[m]
                            d, a = readers_before(b, m + 1)
                            with_prev = (d - dve_jobs) if by else (a - act_jobs)
                            pe.wait_ge(job_used_dve if by else job_used, with_prev)
                        if job[0] == "turn":
                            a = job[1]
                            for t in range(TILES):
                                mm = nc.tensor.transpose(bank[:, t * P:(t + 1) * P], xn[:, t, a * P:(a + 1) * P], ident[:])
                        elif job[0] == "q":
                            if job[1] == 0:
                                pe.wait_ge(job_used_dve, b * dve_jobs + HALVES)
                            for c in range(HALVES):
                                mm = nc.tensor.matmul(bank, wq_s[:, c, job[1] * P:(job[1] + 1) * P], xnt[:, c], start=c == 0, stop=c == HALVES - 1)
                        elif job[0] == "k":
                            if job[1:] == (0, 0):
                                pe.wait_ge(ctx_loaded[u], 16 * (g + 1))
                            lo, hi = KEY_PIECES[job[2]]
                            for c in range(HALVES):
                                mm = nc.tensor.matmul(bank[:, 0:hi - lo], wk_s[:, c, job[1] * P:(job[1] + 1) * P], ct[:, u, c, lo:hi], start=c == 0, stop=c == HALVES - 1)
                        else:
                            lo, hi = job[1] * P, min(job[1] * P + P, KEYS)
                            for c in range(HALVES):
                                mm = nc.tensor.matmul(bank[0:hi - lo, 0:DIM], ct[:, u, c, lo:hi], wv_s[:, c], start=c == 0, stop=c == HALVES - 1)
                        mm.then_inc(job_made, 1)

            pair(0)
            with pe.Fori(1, BATCH // 2) as g:
                pair(g)

        @block.scalar
        def _(act):
            act.wait_ge(weights, 16 * 9)
            nc.scalar.mul(bqs[:], bq_s[:], SCALE).then_inc(consts, 1)
            act.wait_ge(consts, 1)
            with act.Fori(0, BATCH) as b:
                act.wait_ge(stats_done, b + 1)
                nc.scalar.activation(std[:], veps[:], ACT.Sqrt).then_inc(std_done, 1)
                for n, job in enumerate(jobs):
                    if job[0] == "k":
                        a, c = job[1:]
                        if (a, c) == (0, 0):
                            act.wait_ge(k_rest, b)
                        lo, hi = KEY_PIECES[c]
                        act.wait_ge(job_made, NJ * b + n + 1)
                        nc.scalar.activation(kf[:, a, lo:hi], ring[:, n % RING, 0:hi - lo], ACT.Identity, bias=bk_s[:, a:a + 1]).then_inc(job_used, 1)
                        if (a, c) == (HALVES - 1, len(KEY_PIECES) - 1):
                            act.wait_ge(job_used, readers_before(b, n + 1)[1])
                            act.wait_ge(k_stored, 48 * b)
                            nc.scalar.copy(ks[:, 0], kf[:]).then_inc(k_high, 1)
                    elif job[0] == "q":
                        a = job[1]
                        if a == 0:
                            act.wait_ge(q_rest, b)
                        act.wait_ge(job_made, NJ * b + n + 1)
                        nc.scalar.activation(qf[:, a], ring[:, n % RING], ACT.Identity, bias=bqs[:, a:a + 1], scale=SCALE).then_inc(job_used, 1)
                        if a == HALVES - 1:
                            act.wait_ge(job_used, readers_before(b, n + 1)[1])
                            act.wait_ge(q_stored, 48 * b)
                            nc.scalar.copy(qs[:, 0], qf[:]).then_inc(q_high, 1)

        @block.gpsimd
        def _(pool):
            with pool.Fori(0, BATCH) as b:
                pool.wait_ge(k_high, b + 1)
                pool.wait_ge(k_split, b)
                nc.gpsimd.tensor_tensor(kr[:], kf[:], ks[:, 0], ALU.subtract).then_inc(k_rest, 1)
                pool.wait_ge(q_high, b + 1)
                pool.wait_ge(q_split, b)
                nc.gpsimd.tensor_tensor(qr[:], qf[:], qs[:, 0], ALU.subtract).then_inc(q_rest, 1)

        @block.vector
        def _(dve):
            dve.wait_ge(weights, 16 * 9)
            LINKS = 5 + 2

            def batch(b, u, g):
                made = [LINKS * b]

                def link(ins):
                    made[0] = made[0] + 1
                    ins.then_inc(chain, 1)
                    dve.wait_ge(chain, made[0])

                dve.wait_ge(x_loaded[u], 16 * (g + 1))
                for t in range(TILES):
                    ins = nc.vector.bn_stats(stats[:, t], xt[:, u, t])
                link(ins)
                dve.sem_inc(passed, 1)
                for t in range(TILES):
                    ins = nc.vector.bn_aggr(moments[:, t], stats[:, t])
                link(ins)
                nc.vector.tensor_scalar(veps[:], moments[:, :, 1], EPS, None, ALU.add).then_inc(stats_done, 1)
                dve.wait_ge(std_done, b + 1)
                link(nc.vector.reciprocal(rstd[:], std[:]))
                link(nc.vector.tensor_tensor(fix[:], rstd[:], rstd[:], ALU.mult))
                link(nc.vector.tensor_tensor(fix[:], fix[:], veps[:], ALU.mult))
                link(nc.vector.tensor_scalar(fix[:], fix[:], -0.5, 1.5, ALU.mult, ALU.add))
                link(nc.vector.tensor_tensor(rstd[:], rstd[:], fix[:], ALU.mult))
                for t in range(TILES):
                    nc.vector.tensor_scalar(xn[:, t], xt[:, u, t], moments[:, t, 0:1], rstd[:, t:t + 1], ALU.subtract, ALU.mult).then_inc(normed, 1)
                for n, job in enumerate(jobs):
                    if job[0] == "turn":
                        if job[1] == 0:
                            dve.wait_ge(q_high, b)
                        dve.wait_ge(job_made, NJ * b + n + 1)
                        nc.vector.tensor_copy(xnt[:, job[1]], ring[:, n % RING]).then_inc(job_used_dve, 1)
                for n, job in enumerate(jobs):
                    if job[0] == "v":
                        c = job[1]
                        rows = P if c < KCHUNKS - 1 else LAST_KEYS
                        if c == 0:
                            dve.wait_ge(v_stored, 32 * b)
                        dve.wait_ge(job_made, NJ * b + n + 1)
                        nc.vector.tensor_tensor(vt[0:rows, :, c, :], ring[0:rows, n % RING, 0:DIM].rearrange("p (h d) -> p h d", h=HEADS),
                                                bv_s[0:rows].rearrange("p (h d) -> p h d", h=HEADS), ALU.add).then_inc(job_used_dve, 1)
                for rest, high, mid, split, r, s in ((q_rest, q_high, q_mid, q_split, qr, qs), (k_rest, k_high, k_mid, k_split, kr, ks)):
                    dve.wait_ge(rest, b + 1)
                    nc.vector.tensor_copy(s[:, 1], r[:]).then_inc(mid, 1)
                    dve.wait_ge(mid, b + 1)
                    nc.vector.tensor_tensor(s[:, 2], r[:], s[:, 1], ALU.subtract).then_inc(split, 1)

            with dve.Fori(0, BATCH // 2) as g:
                for u in range(2):
                    batch(2 * g + u, u, g)


def attend_program(nc, q_parts, k_parts, v_heads, ident_in, o_parts):
    N = BATCH * HEADS
    U = 6
    SLOTS = 3
    RING = 3
    LAG = 3
    S_PIECES = [(t, lo, min(lo + 2 * BANK, KEYS)) for t in range(TILES) for lo in range(0, KEYS, 2 * BANK)]
    T_PIECES = [range(c, min(c + 2, KCHUNKS)) for c in range(0, KCHUNKS, 2)]
    NS, NT = len(S_PIECES), len(T_PIECES)
    assert (NS + NT) % RING == 0 and U % SLOTS == 0 and U % 2 == 0

    def groups(do_s, do_t):
        place, out = 0, []
        for g in range(TILES):
            own = []
            for kind, n, there in [("s", 2 * g, do_s), ("s", 2 * g + 1, do_s)] + [("t", k, do_t) for k in range(2 * g, min(2 * g + 2, NT))]:
                if there:
                    own.append((kind, n, place))
                    place += 1
            out.append(own)
        return out

    def before(i):
        if isinstance(i, int):
            return NS * min(i, N) + NT * min(max(0, i - LAG), N)
        return i * (NS + NT) - NT * LAG

    def slot(i, place):
        return ((before(i) if isinstance(i, int) else -NT * LAG) + place) % RING

    def score_place(n, do_t):
        return next(p for own in groups(True, do_t) for kind, m, p in own if kind == "s" and m == n)

    def walk(engine, step):
        for i in range(U):
            step(i, i)
        with engine.Fori(1, N // U) as g:
            for u in range(U):
                step(g * U + u, u)
        for i in range(N // U * U, N + LAG + 1):
            step(i, i % U)

    def has(i, lag):
        return not isinstance(i, int) or 0 <= i - lag < N

    with ExitStack() as ctx:
        def sb(name, shape, dt=F32):
            return ctx.enter_context(nc.sbuf_tensor("a_" + name, shape, dt))

        def sem(name):
            return ctx.enter_context(nc.semaphore("a_" + name))

        ring = ctx.enter_context(nc.psum_tensor("a_ring", [P, RING, 2 * BANK], F32))
        out_ps = ctx.enter_context(nc.psum_tensor("a_out", [P, BANK], F32))
        turn_ps = ctx.enter_context(nc.psum_tensor("a_turn", [P, BANK], F32))

        k_st = sb("k", [P, U, KEYS], BF16)
        q_st = sb("q", [P, U, QUERIES], BF16)
        v_st = sb("v", [P, U, KCHUNKS, HEAD_DIM])
        scores = sb("scores", [P, SLOTS, TILES, KEYS])
        attn = sb("attn", [P, NT, 2 * BANK])
        o_sb = sb("o", [P, QUERIES])
        cand = sb("cand", [P, SLOTS, TILES, CHUNKS, 8])
        junk, junk2 = sb("junk", [P, KEYS]), sb("junk2", [P, KEYS])
        junk_act = sb("junk_act", [P, TILES, CAND])
        junk_act0 = sb("junk_act0", [P, TILES, CHUNKS * SECOND])
        zeros = sb("zeros", [P, 1])
        ident_f = sb("ident_f", [P, P])
        ident = sb("ident", [P, P], BF16)
        ones = sb("ones", [P, 1], BF16)
        ntau = sb("ntau", [P, 2, TILES])
        ntop = sb("ntop", [P, TILES])
        excess = sb("excess", [P, 2, ROUNDS, TILES])
        own_excess = sb("own_excess", [P, TILES])
        count = sb("count", [P, TILES])
        model = sb("model", [P, TILES])
        inv = sb("inv", [P, 2, TILES])
        move = sb("move", [P, 2, TILES])
        w1, w2, w3 = (sb(n, [P, TILES]) for n in ("w1", "w2", "w3"))
        miss = sb("miss", [P, TILES])
        unit = sb("unit", [P, TILES])
        bad = sb("bad", [P, TILES], BF16)
        weigh = sb("weigh", [P, TILES])
        tile_bits = sb("tile_bits", [1, TILES])
        bit_sum = sb("bit_sum", [1, 1])
        bad_bits = sb("bad_bits", [1, 1], I32)
        g_excess, g_count, g_over1, g_miss, g_move = (sb(n, [P, 1]) for n in ("g_excess", "g_count", "g_over1", "g_miss", "g_move"))
        over1 = sb("over1", [P, TILES])
        rest = sb("rest", [P, TILES])
        split = sb("split", [P, TILES, TAU_ROWS], BF16)
        flag = sb("flag", [P, 32])
        flag_t = sb("flag_t", [P, 32])
        flag_row = sb("flag_row", [1, 4, 32])
        flag_i = sb("flag_i", [1, 1], I32)

        loaded = [sem(f"loaded{u}") for u in range(U)]
        ident_loaded = sem("ident_loaded")
        setup = sem("setup")
        piece_made = sem("piece_made")
        piece_used = sem("piece_used")
        products = sem("products")
        out_copied = sem("out_copied")
        out_stored = sem("out_stored")
        cand_made = sem("cand_made")
        tau_tried = sem("tau_tried")
        tau_tried_last = sem("tau_tried_last")
        inv_made = sem("inv_made")
        stepped = sem("stepped")
        excess_made = sem("excess_made")
        bad_ready = sem("bad_ready")
        bad_counted = sem("bad_counted")
        settled = sem("settled")
        tau_split = sem("tau_split")
        pool_chain = sem("pool_chain")
        tau_turned = sem("tau_turned")
        tau_in_q = sem("tau_in_q")
        chain = sem("chain")
        passed, passed_pool = sem("passed"), sem("passed_pool")
        general = sem("general")
        SETUP = 6 + TILES
        FIRST_ROUNDS = 3
        LOADS = len(K_PARTS) + len(Q_PARTS) + 2

        block = ctx.enter_context(nc.Block())

        @block.sync
        def _(sp):
            sp.dma_start(ident_f[:], ident_in).then_inc(ident_loaded, 16)

            def load(i, u):
                for parts, st, run in ((K_PARTS, k_st, k_parts), (Q_PARTS, q_st, q_parts)):
                    for n, s in enumerate(parts):
                        sp.dma_start(st[n * HEAD_DIM:(n + 1) * HEAD_DIM, u], run[s, bass.ds(i * HEAD_DIM, HEAD_DIM)]).then_inc(loaded[u], 16)
                sp.dma_start(v_st[:, u, 0:KCHUNKS - 1], v_heads[i][:, 0:KCHUNKS - 1]).then_inc(loaded[u], 16)
                sp.dma_start(v_st[0:LAST_KEYS, u, KCHUNKS - 1:], v_heads[i][0:LAST_KEYS, KCHUNKS - 1:]).then_inc(loaded[u], 16)

            def store(i):
                sp.wait_ge(out_copied, i + 1)
                for s in range(4):
                    sp.dma_start(o_parts[s, bass.ds(i * HEAD_DIM, HEAD_DIM)], o_sb[32 * s:32 * s + HEAD_DIM]).then_inc(out_stored, 16)

            for i in range(U):
                load(i, i)
            with sp.Fori(0, N // U - 1) as g:
                for u in range(U):
                    i = g * U + u
                    sp.wait_ge(products, NT * (i + 1))
                    load(i + U, u)
                    store(i)
            for i in range((N // U - 1) * U, N):
                if i + U < N:
                    sp.wait_ge(products, NT * (i + 1))
                    load(i + U, i % U)
                store(i)
            sp.wait_ge(out_stored, 64 * N)

        @block.tensor
        def _(pe):
            pe.wait_ge(setup, SETUP)

            def multiply(i, k, u, t_place):
                pe.wait_ge(piece_used, t_place + 1)
                if k == 0:
                    pe.wait_ge(out_copied, i)
                for c in T_PIECES[k]:
                    rows = P if c < KCHUNKS - 1 else LAST_KEYS
                    at = 32 * (c % 4)
                    mm = nc.tensor.matmul(out_ps[at:at + HEAD_DIM], v_st[0:rows, u, c], attn[0:rows, k, (c % 2) * BANK:(c % 2 + 1) * BANK],
                                          start=c < 4, stop=c >= KCHUNKS - 4)
                mm.then_inc(products, 1)

            group_now = [None]

            def i_group(i, u):
                return group_now[0]

            def before_prev(i):
                return before(i - 1) if isinstance(i, int) else before(i) - NS - NT

            def count_bad(i):
                pe.wait_ge(bad_ready, i + 1)
                nc.tensor.matmul(turn_ps[0:1, 0:TILES], ones[:], bad[:], start=True, stop=True).then_inc(bad_counted, 1)

            def turn_tau(i):
                pe.wait_ge(tau_split, i + 1)
                if not isinstance(i, int) or i >= 1:
                    pe.wait_ge(tau_in_q, i)
                for t in range(TILES):
                    mm = nc.tensor.matmul(turn_ps[SCORE_ROWS:SCORE_ROWS + TAU_ROWS, t * P:(t + 1) * P], split[:, t], ident[:], start=True, stop=True)
                mm.then_inc(tau_turned, 1)

            def step(i, u):
                do_s, do_t = has(i, 0), has(i, LAG)
                ut = (u - LAG) % U
                if do_s:
                    pe.wait_ge(loaded[u], 16 * LOADS * ((i // U if isinstance(i, int) else i_group(i, u)) + 1))
                if do_t:
                    pe.wait_ge(tau_in_q, i - LAG + 1)
                order = groups(do_s, do_t)
                for g, own in enumerate(order):
                    for kind, n, place in own:
                        seq = before(i) + place
                        if not isinstance(i, int) or seq >= RING:
                            pe.wait_ge(piece_used, seq - RING + 1)
                        at = ring[:, slot(i, place)]
                        if kind == "s":
                            t, lo, hi = S_PIECES[n]
                            for c in range(lo, hi, BANK):
                                w = min(BANK, hi - c)
                                mm = nc.tensor.matmul(at[:, c - lo:c - lo + w], q_st[0:SCORE_ROWS, u, t * P:(t + 1) * P], k_st[0:SCORE_ROWS, u, c:c + w], start=True, stop=True)
                        else:
                            for m, c in enumerate(T_PIECES[n]):
                                rows = P if c < KCHUNKS - 1 else LAST_KEYS
                                mm = nc.tensor.matmul(at[0:rows, m * BANK:(m + 1) * BANK], k_st[0:SCORE_ROWS + TAU_ROWS, ut, c * P:c * P + rows],
                                                      q_st[0:SCORE_ROWS + TAU_ROWS, ut], start=True, stop=True)
                        mm.then_inc(piece_made, 1)
                    if g == 0:
                        if has(i, LAG + 1):
                            last = NT - 1
                            p = next(p for o in groups(has(i, 1), has(i, LAG + 1)) for kd, n, p in o if (kd, n) == ("t", last))
                            multiply(i - LAG - 1, last, (ut - 1) % U, before_prev(i) + p)
                    else:
                        for kd, n, p in order[g - 1]:
                            if kd == "t":
                                multiply(i - LAG, n, ut, before(i) + p)
                    if g == 2 and has(i, 2):
                        count_bad(i - 2)
                    if g == 3 and has(i, 2):
                        turn_tau(i - 2)
            for i in range(U):
                step(i, i)
            with pe.Fori(1, N // U) as g:
                group_now[0] = g
                for u in range(U):
                    step(g * U + u, u)
            for i in range(N // U * U, N + LAG + 1):
                step(i, i % U)

        @block.scalar
        def _(act):
            act.wait_ge(setup, SETUP)

            def measure_excess(i, u, r):
                if r < FIRST_ROUNDS:
                    act.wait_ge(tau_tried, FIRST_ROUNDS * i + r + 1)
                else:
                    act.wait_ge(tau_tried_last, (ROUNDS - FIRST_ROUNDS) * i + r - FIRST_ROUNDS + 1)
                for t in range(TILES):
                    w, into = (SECOND, junk_act0) if r == 0 else (8, junk_act)
                    ins = nc.scalar.activation(into[:, t].rearrange("p (a b) -> p a b", a=CHUNKS), cand[:, u % SLOTS, t, :, 0:w], ACT.Relu,
                                               bias=ntau[:, u % 2, t:t + 1], accum_out=excess[:, u % 2, r, t:t + 1])
                ins.then_inc(excess_made, 1)

            def step(i, u):
                do_s, do_t = has(i, 0), has(i, LAG)
                ut = (u - LAG) % U
                if do_t:
                    act.wait_ge(tau_turned, i - LAG + 1)
                    nc.scalar.copy(q_st[SCORE_ROWS:SCORE_ROWS + TAU_ROWS, ut], turn_ps[SCORE_ROWS:SCORE_ROWS + TAU_ROWS]).then_inc(tau_in_q, 1)
                if do_s and (not isinstance(i, int) or i >= SLOTS):
                    act.wait_ge(settled, i - SLOTS + 1)
                for g, own in enumerate(groups(do_s, do_t)):
                    for kind, n, place in own:
                        seq = before(i) + place
                        at = ring[:, slot(i, place)]
                        if kind == "t" and (not isinstance(i, int) or i > LAG):
                            act.wait_ge(products, NT * (i - LAG - 1) + n + 1)
                        act.wait_ge(piece_made, seq + 1)
                        if kind == "s":
                            t, lo, hi = S_PIECES[n]
                            nc.scalar.copy(scores[:, u % SLOTS, t, lo:hi], at[:, 0:hi - lo]).then_inc(piece_used, 1)
                        else:
                            rows = P if T_PIECES[n][-1] < KCHUNKS - 1 else LAST_KEYS
                            w = len(T_PIECES[n]) * BANK
                            nc.scalar.activation(attn[0:rows, n, 0:w], at[0:rows, 0:w], ACT.Relu).then_inc(piece_used, 1)
                    if g == 0 and has(i, LAG + 1):
                        act.wait_ge(products, NT * (i - LAG))
                        if not isinstance(i, int) or i > LAG + 1:
                            act.wait_ge(out_stored, 64 * (i - LAG - 1))
                        nc.scalar.copy(o_sb[:], out_ps[:]).then_inc(out_copied, 1)
                    if g < 2 and has(i, 2):
                        measure_excess(i - 2, (u - 2) % U, FIRST_ROUNDS + g)
                    if g > 0 and has(i, 1):
                        measure_excess(i - 1, (u - 1) % U, g - 1)

            walk(act, step)

        @block.vector
        def _(dve):
            nc.vector.memset(k_st[SCORE_ROWS:SCORE_ROWS + TAU_ROWS], 1.0).then_inc(setup, 1)
            nc.vector.memset(ones[:], 1.0).then_inc(setup, 1)
            nc.vector.memset(zeros[:], 0.0).then_inc(setup, 1)
            nc.vector.memset(unit[:], 1.0).then_inc(setup, 1)
            for t in range(TILES):
                nc.vector.memset(weigh[:, t:t + 1], 2.0 ** t).then_inc(setup, 1)
            nc.vector.memset(out_ps[:], 0.0).then_inc(setup, 1)
            nc.vector.memset(flag[:], 0.0).then_inc(chain, 1)
            dve.wait_ge(ident_loaded, 16)
            nc.vector.tensor_copy(ident[:], ident_f[:]).then_inc(setup, 1)
            dve.wait_ge(setup, SETUP)
            dve.wait_ge(chain, 1)
            unsettled = dve.alloc_register("unsettled")
            bits = dve.alloc_register("bits")
            steps_left = dve.alloc_register("steps_left")
            V = nc.vector

            def view(tile, values, width, n):
                flat = tile[:, n * width:(n + 1) * width]
                return flat.rearrange("p (a b) -> p a b", a=CHUNKS) if len(values.shape) == 3 else flat

            def zeros_like(values):
                return (zeros[:].unsqueeze(2) if len(values.shape) == 3 else zeros[:]).broadcast_to(list(values.shape))

            def measure_own(t, values, width, nt):
                return V.scalar_tensor_tensor(out=view(junk, values, width, TILES + t), in0=values, scalar=nt[:, t:t + 1], in1=zeros_like(values), op0=ALU.add, op1=ALU.max,
                                              accum_out=own_excess[:, t:t + 1])

            def measure_count(t, values, width, nt):
                return V.scalar_tensor_tensor(out=view(junk, values, width, t), in0=values, scalar=nt[:, t:t + 1], in1=zeros_like(values), op0=ALU.add, op1=ALU.is_gt,
                                              accum_out=count[:, t:t + 1])


            def guess(link, e, nt):
                V.scalar_tensor_tensor(out=w2[:], in0=e, scalar=1.0, in1=e, op0=ALU.subtract, op1=ALU.mult)
                yield from link(V.tensor_scalar(w1[:], e, 1.0, None, ALU.add))
                yield from link(V.scalar_tensor_tensor(out=w1[:], in0=count[:], scalar=1.0, in1=w1[:], op0=ALU.max, op1=ALU.mult))
                yield from link(V.reciprocal(w1[:], w1[:]))
                yield from link(V.scalar_tensor_tensor(out=w3[:], in0=w2[:], scalar=-2.0, in1=w1[:], op0=ALU.mult, op1=ALU.mult))
                yield from link(V.tensor_tensor(nt, nt, w3[:], ALU.add))

            def start(i, u, link):
                c, nt = cand[:, u % SLOTS], ntau[:, u % 2]
                if not isinstance(i, int) or i >= 2:
                    dve.wait_ge(tau_split, i - 1)
                    dve.sem_inc(passed, 1)
                V.tensor_reduce(ntop[:], c[:, :, :, 0], AX.X, ALU.max, negate=True)
                yield from link(V.tensor_reduce(w1[:], c[:, :, :, 0], AX.X, ALU.add))
                yield from link(V.tensor_scalar(nt, w1[:], -1.0 / CHUNKS, None, ALU.mult))
                for t in range(TILES):
                    measure_own(t, c[:, t, :, 0:FIRST], CHUNKS * FIRST, nt)
                    ins = measure_count(t, c[:, t, :, 0:FIRST], CHUNKS * FIRST, nt)
                yield from link(ins)
                yield from guess(link, own_excess[:], nt)
                for t in range(TILES):
                    ins = measure_count(t, c[:, t, :, 0:SECOND], CHUNKS * SECOND, nt)
                ins.then_inc(tau_tried, 1)
                dve.wait_ge(tau_tried, FIRST_ROUNDS * i + 1)

            def second(i, u, link):
                e, nt = excess[:, u % 2, 0], ntau[:, u % 2]
                dve.wait_ge(excess_made, ROUNDS * i + 1)
                yield from guess(link, e, nt)
                yield from link(V.scalar_tensor_tensor(out=nt, in0=ntop[:], scalar=1.0, in1=nt, op0=ALU.add, op1=ALU.min))
                V.scalar_tensor_tensor(out=nt, in0=ntop[:], scalar=1.0 / KEYS, in1=nt, op0=ALU.add, op1=ALU.max).then_inc(tau_tried, 1)
                yield from link(V.tensor_scalar(model[:], e, 0.25, 4.0, ALU.max, ALU.min))
                yield from link(V.scalar_tensor_tensor(out=w2[:], in0=e, scalar=1.0, in1=w1[:], op0=ALU.add, op1=ALU.mult))
                yield from link(V.tensor_tensor(model[:], model[:], w2[:], ALU.mult))

            def third(i, u, link):
                e, nt, mv = excess[:, u % 2, 1], ntau[:, u % 2], move[:, u % 2]
                dve.wait_ge(excess_made, ROUNDS * i + 2)
                yield from link(V.tensor_scalar(w1[:], e, 1.0, None, ALU.add))
                yield from link(V.reciprocal(w1[:], w1[:]))
                yield from link(V.scalar_tensor_tensor(out=w2[:], in0=e, scalar=1.0, in1=model[:], op0=ALU.subtract, op1=ALU.mult))
                yield from link(V.scalar_tensor_tensor(out=mv, in0=w2[:], scalar=2.0, in1=w1[:], op0=ALU.mult, op1=ALU.mult))
                V.tensor_tensor(nt, nt, mv, ALU.subtract).then_inc(tau_tried, 1)
                yield from link(V.tensor_tensor(w3[:], mv, mv, ALU.mult))

            def slope(i, u, link):
                e, mv, iv = excess[:, u % 2], move[:, u % 2], inv[:, u % 2]
                dve.wait_ge(excess_made, ROUNDS * i + 3)
                yield from link(V.tensor_tensor(w1[:], e[:, 1], e[:, 2], ALU.subtract))
                yield from link(V.tensor_tensor(w1[:], w1[:], mv, ALU.mult))
                yield from link(V.tensor_scalar(w1[:], w1[:], 1e-30, None, ALU.max))
                yield from link(V.reciprocal(w1[:], w1[:]))
                yield from link(V.tensor_tensor(w1[:], w1[:], w3[:], ALU.mult))
                yield from link(V.scalar_tensor_tensor(out=w1[:], in0=model[:], scalar=0.5, in1=w1[:], op0=ALU.mult, op1=ALU.max))
                V.scalar_tensor_tensor(out=iv, in0=model[:], scalar=2.0, in1=w1[:], op0=ALU.mult, op1=ALU.min).then_inc(inv_made, 1)
                dve.wait_ge(inv_made, i + 1)

            def judge(i, u, link):
                yield from link(V.tensor_reduce(w1[:], cand[:, u % SLOTS, :, :, 7], AX.X, ALU.max))
                dve.wait_ge(stepped, i + 1)
                yield from link(V.tensor_tensor(w1[:], w1[:], ntau[:, u % 2], ALU.add))
                yield from link(V.tensor_scalar(w1[:], w1[:], 0.0, None, ALU.is_gt))
                V.scalar_tensor_tensor(out=bad[:], in0=miss[:], scalar=EXACT ** 2, in1=w1[:], op0=ALU.is_gt, op1=ALU.max).then_inc(bad_ready, 1)
                dve.wait_ge(bad_ready, i + 1)

            FIRST_LINKS = (2 + 1 + 5) + (6 + 3) + 5 + 6
            LAST_LINKS = 3 + 2

            def links_before(i):
                if isinstance(i, int):
                    return 1 + FIRST_LINKS * min(max(0, i - 1), N) + LAST_LINKS * min(max(0, i - 2), N)
                return i * (FIRST_LINKS + LAST_LINKS) + (1 - FIRST_LINKS - 2 * LAST_LINKS)

            def general_path(sc, nt):
                dve.sem_clear(general)
                links = [0]

                def link(ins):
                    links[0] += 1
                    ins.then_inc(general, 1)
                    dve.wait_ge(general, links[0])

                every = zeros[:].broadcast_to([P, KEYS])
                V.scalar_tensor_tensor(out=junk[:], in0=sc, scalar=nt, in1=every, op0=ALU.add, op1=ALU.max, accum_out=g_excess[:]).then_inc(general, 1)
                links[0] += 1
                link(V.scalar_tensor_tensor(out=junk2[:], in0=sc, scalar=nt, in1=every, op0=ALU.add, op1=ALU.is_gt, accum_out=g_count[:]))
                V.tensor_scalar(g_over1[:], g_excess[:], 1.0, None, ALU.subtract).then_inc(general, 1)
                links[0] += 1
                link(V.tensor_scalar(g_count[:], g_count[:], 1.0, None, ALU.max))
                V.tensor_tensor(g_miss[:], g_over1[:], g_over1[:], ALU.mult).then_inc(general, 1)
                links[0] += 1
                link(V.reciprocal(g_count[:], g_count[:]))
                V.tensor_scalar(flag[:, 0:1], g_miss[:], EXACT ** 2, None, ALU.is_gt).then_inc(general, 1)
                links[0] += 1
                link(V.tensor_tensor(g_move[:], g_over1[:], g_count[:], ALU.mult))
                V.tensor_tensor(nt, nt, g_move[:], ALU.subtract).then_inc(general, 1)
                links[0] += 1
                link(V.transpose(flag_t[:], flag[:]))
                for q in range(P // 32):
                    ins = V.tensor_copy(flag_row[:, q], flag_t[32 * q:32 * q + 1])
                link(ins)
                with nc.allow_low_precision(reason="counts up to 128 are exact as integers"):
                    link(V.tensor_reduce(flag_i[:], flag_row[:], AX.XY, ALU.add))
                dve.reg_load(unsettled, flag_i[:])
                dve.reg_sub(steps_left, steps_left, 1)
                dve.reg_mul(unsettled, unsettled, steps_left)

            def settle(i, u, link):
                dve.wait_ge(bad_counted, i + 1)
                yield from link(V.scalar_tensor_tensor(out=tile_bits[:], in0=turn_ps[0:1, 0:TILES], scalar=1.0, in1=weigh[0:1], op0=ALU.min, op1=ALU.mult, accum_out=bit_sum[:]))
                yield from link(V.tensor_copy(bad_bits[:], bit_sum[:]))
                dve.sem_inc(passed, 1)
                dve.reg_load(bits, bad_bits[:])
                with dve.If(dve.snap(bits) > 0):
                    for t in range(TILES):
                        dve.reg_mod(unsettled, bits, 2)
                        dve.reg_div(bits, bits, 2)
                        with dve.If(dve.snap(unsettled) > 0):
                            dve.reg_mov(steps_left, GENERAL_STEPS)
                            with dve.While(lambda: dve.snap(unsettled) > 0):
                                general_path(scores[:, u % SLOTS, t], ntau[:, u % 2, t:t + 1])
                dve.sem_inc(settled, 1)

            def step(i, u):
                made = [links_before(i)]

                def link(ins):
                    made[0] = made[0] + 1
                    ins.then_inc(chain, 1)
                    own = made[0]
                    yield
                    dve.wait_ge(chain, own)

                def beside(t):
                    last, prev = (u - 2) % U, (u - 1) % U
                    if t == 0 and has(i, 1):
                        dve.wait_ge(cand_made, i)
                        yield from start(i - 1, prev, link)
                    if t == 1 and has(i, 1):
                        yield from second(i - 1, prev, link)
                    if t == 1 and has(i, 2):
                        yield from judge(i - 2, last, link)
                    if t == 2 and has(i, 1):
                        yield from third(i - 1, prev, link)
                    if t == 2 and has(i, 2):
                        yield from settle(i - 2, last, link)
                    if t == 3 and has(i, 1):
                        yield from slope(i - 1, prev, link)
                    dve.sem_inc(passed, 1)

                for t in range(TILES):
                    side = beside(t)
                    if has(i, 0):
                        dve.wait_ge(piece_used, before(i) + score_place(2 * t + 1, has(i, LAG)) + 1)
                        dve.sem_inc(passed, 1)
                        for c, (lo, hi) in enumerate(RUNS):
                            ins = V.max(cand[:, u % SLOTS, t, c], scores[:, u % SLOTS, t, lo:hi])
                            if c % 2:
                                next(side, None)
                        if t == TILES - 1:
                            ins.then_inc(cand_made, 1)
                    for _ in side:
                        pass

            walk(dve, step)

        @block.gpsimd
        def _(pool):
            pool.wait_ge(setup, SETUP)
            G = nc.gpsimd
            LINKS = 2 + 2 + 3 + 3

            def step(i, u):
                made = [LINKS * i]
                nt, mv, iv = ntau[:, u % 2], move[:, u % 2], inv[:, u % 2]

                def link(ins):
                    made[0] = made[0] + 1
                    ins.then_inc(pool_chain, 1)
                    pool.wait_ge(pool_chain, made[0])
                    pool.sem_inc(passed_pool, 1)

                for r in range(FIRST_ROUNDS - 1, ROUNDS):
                    e = excess[:, u % 2, r]
                    if r == FIRST_ROUNDS - 1:
                        pool.wait_ge(inv_made, i + 1)
                        pool.sem_inc(passed_pool, 1)
                    else:
                        pool.wait_ge(excess_made, ROUNDS * i + r + 1)
                        pool.sem_inc(passed_pool, 1)
                    link(G.tensor_tensor(over1[:], e, unit[:], ALU.subtract))
                    link(G.tensor_tensor(mv, over1[:], iv, ALU.mult))
                    if r < ROUNDS - 1:
                        G.tensor_tensor(nt, nt, mv, ALU.subtract).then_inc(tau_tried_last, 1)
                        pool.wait_ge(tau_tried_last, (ROUNDS - FIRST_ROUNDS) * i + r - FIRST_ROUNDS + 2)
                        pool.sem_inc(passed_pool, 1)
                    else:
                        link(G.tensor_tensor(nt, nt, mv, ALU.subtract))
                        G.tensor_tensor(miss[:], over1[:], over1[:], ALU.mult).then_inc(stepped, 1)
                pool.wait_ge(settled, i + 1)
                pool.sem_inc(passed_pool, 1)
                pool.wait_ge(tau_turned, i)
                pool.sem_inc(passed_pool, 1)
                link(G.tensor_copy(split[:, :, 0], nt))
                link(G.tensor_tensor(rest[:], nt, split[:, :, 0], ALU.subtract))
                link(G.tensor_copy(split[:, :, 1], rest[:]))
                G.tensor_tensor(split[:, :, 2], rest[:], split[:, :, 1], ALU.subtract).then_inc(tau_split, 1)

            with pool.Fori(0, N // 2) as g:
                for u in range(2):
                    step(2 * g + u, u)


def experts_program(nc, x, g_attn, g_ffn, wo, bo, o_parts, router_w, w_in, b_in, w_out, b_out, ident_in, out):
    with ExitStack() as ctx:
        def sb(name, shape, dt=F32):
            return ctx.enter_context(nc.sbuf_tensor("e_" + name, shape, dt))

        def sem(name):
            return ctx.enter_context(nc.semaphore("e_" + name))

        def ps(name, banks):
            return ctx.enter_context(nc.psum_tensor("e_" + name, [P, banks, BANK], F32))

        hid_ps = ps("hid_ps", 4)
        y_ps = ps("y_ps", 2)
        turn_ps = ps("turn_ps", 2)
        y_tile = [y_ps[:, t // 2, (t % 2) * DIM:(t % 2 + 1) * DIM] for t in range(TILES)]

        win_s = sb("w_in", [P, EXPERTS, HALVES, HIDDEN])
        wout_s = sb("w_out", [P, EXPERTS, HALVES, DIM])
        bin_s = sb("b_in", [P, EXPERTS, HALVES])
        bout_s = sb("b_out", [EXPERTS, DIM])
        wo_s = sb("wo", [P, HALVES, DIM])
        wr_s = sb("router", [P, HALVES, EXPERTS])
        bo_s = sb("bo", [P, DIM])
        ident = sb("ident", [P, P])
        g_s = sb("g", [P, 2])
        gates = sb("gates", [P, 2])
        places = sb("places", [P, EXPERTS])
        places_i = sb("places_i", [P, EXPERTS], I32)
        x_s = sb("x", [P, TILES, DIM])
        o_s = sb("o", [P, HALVES, 4, QUERIES])
        osum = sb("osum", [P, HALVES, QUERIES])
        x2 = sb("x2", [P, TILES, DIM])
        stats = sb("stats", [P, TILES, 6])
        moments = sb("moments", [P, TILES, 2])
        veps, std, rstd, fix = (sb(n, [P, TILES]) for n in ("veps", "std", "rstd", "fix"))
        xn = sb("xn", [P, TILES, DIM])
        xnt = sb("xnt", [P, HALVES, QUERIES])
        logits = sb("logits", [P, TILES, EXPERTS])
        best = sb("best", [P, TILES, 8])
        best_i = sb("best_i", [P, TILES, 8], U32)
        best_f = sb("best_f", [P, TILES, 8])
        nbest = sb("nbest", [P, TILES])
        prob = sb("prob", [P, TILES, EXPERTS])
        mass = sb("mass", [P, TILES])
        rmass = sb("rmass", [P, TILES])
        pick = sb("pick", [P, TILES, EXPERTS])
        pick2 = sb("pick2", [P, TILES, EXPERTS])
        gate = sb("gate", [P, TILES, EXPERTS])
        gate_t = sb("gate_t", [EXPERTS, QUERIES])
        hid = sb("hid", [P, 2, HALVES, QUERIES])
        acc = sb("acc", [P, TILES, DIM])
        res = sb("res", [P, TILES, DIM])

        weights, x_loaded, o_loaded, stored = sem("weights"), sem("x_loaded"), sem("o_loaded"), sem("stored")
        g_tanh = sem("g_tanh")
        places_made = sem("places_made")
        consts = sem("consts")
        chain = sem("chain")
        o_summed = sem("o_summed")
        projected = sem("projected")
        x2_done = sem("x2_done")
        stats_done = sem("stats_done")
        std_done = sem("std_done")
        normed = sem("normed")
        turned = sem("turned")
        xnt_done = sem("xnt_done")
        routed = sem("routed")
        best_done = sem("best_done")
        exp_done = sem("exp_done")
        gate_done = sem("gate_done")
        gate_turned = sem("gate_turned")
        gate_t_done = sem("gate_t_done")
        bias_made = sem("bias_made")
        hid_made = sem("hid_made")
        hid_done = sem("hid_done")
        y_made = sem("y_made")
        passed = sem("passed")
        y_used = sem("y_used")
        finished = sem("finished")
        LOADS = 9 + EXPERTS * HALVES

        block = ctx.enter_context(nc.Block())

        @block.sync
        def _(sp):
            sp.dma_start(win_s[:], w_in.rearrange("e (a p) n -> p e a n", p=P)).then_inc(weights, 16)
            sp.dma_start(wout_s[:], w_out.rearrange("e (a p) n -> p e a n", p=P)).then_inc(weights, 16)
            for e in range(EXPERTS):
                for a in range(HALVES):
                    sp.dma_start(bin_s[:, e, a:a + 1], b_in[e, a * P:(a + 1) * P].rearrange("(p o) -> p o", o=1)).then_inc(weights, 16)
            sp.dma_start(bout_s[:], b_out).then_inc(weights, 16)
            sp.dma_start(wo_s[:], wo.rearrange("(a p) n -> p a n", p=P)).then_inc(weights, 16)
            sp.dma_start(wr_s[:], router_w.rearrange("(a p) n -> p a n", p=P)).then_inc(weights, 16)
            sp.dma_start(bo_s[:], bo.rearrange("(o n) -> o n", o=1).broadcast_to([P, DIM])).then_inc(weights, 16)
            sp.dma_start(ident[:], ident_in).then_inc(weights, 16)
            for n, g in enumerate((g_attn, g_ffn)):
                sp.dma_start(g_s[:, n:n + 1], g.rearrange("(o n) -> o n", o=1).broadcast_to([P, 1])).then_inc(weights, 16)
            with sp.Fori(0, BATCH) as b:
                sp.wait_ge(x2_done, TILES * b)
                sp.dma_start(x_s[:], x[b].rearrange("(t p) d -> p t d", p=P)).then_inc(x_loaded, 16)
                for s in range(4):
                    sp.dma_start(o_s[:, :, s], o_parts[s, bass.ds(b * DIM, DIM)].rearrange("(a p) n -> p a n", p=P)).then_inc(o_loaded, 16)

        @block.gpsimd
        def _(pool):
            nc.gpsimd.iota(places_i[:], pattern=[[1, EXPERTS]], base=0, channel_multiplier=0).then_inc(places_made, 1)
            with pool.Fori(0, BATCH) as b:
                pool.wait_ge(finished, TILES * (b + 1))
                pool.dma_start(out[b].rearrange("(t p) d -> p t d", p=P), res[:]).then_inc(stored, 16)
            pool.wait_ge(stored, 16 * BATCH)

        @block.tensor
        def _(pe):
            pe.wait_ge(weights, 16 * LOADS)
            with pe.Fori(0, BATCH) as b:
                pe.wait_ge(o_summed, b + 1)
                pe.wait_ge(y_used, (EXPERTS + 1) * b)
                for t in range(TILES):
                    for a in range(HALVES):
                        mm = nc.tensor.matmul(y_tile[t], osum[:, a, t * P:(t + 1) * P], wo_s[:, a], start=a == 0, stop=a == HALVES - 1, skip_group_check=True)
                mm.then_inc(projected, 1)
                pe.wait_ge(normed, TILES * (b + 1))
                for a in range(HALVES):
                    for t in range(TILES):
                        mm = nc.tensor.transpose(turn_ps[:, a, t * P:(t + 1) * P], xn[:, t, a * P:(a + 1) * P], ident[:])
                mm.then_inc(turned, 1)
                pe.wait_ge(xnt_done, HALVES * (b + 1))
                for t in range(TILES):
                    for a in range(HALVES):
                        mm = nc.tensor.matmul(turn_ps[:, 0, t * EXPERTS:(t + 1) * EXPERTS], xnt[:, a, t * P:(t + 1) * P], wr_s[:, a], start=a == 0, stop=a == HALVES - 1, skip_group_check=True)
                mm.then_inc(routed, 1)

                def hidden(e):
                    for m in range(HALVES):
                        n = e * HALVES + m
                        pe.wait_ge(hid_done, HALVES * EXPERTS * b + n - 2 * HALVES + 1) if n >= 2 * HALVES else pe.wait_ge(hid_done, HALVES * EXPERTS * b)
                        for a in range(HALVES):
                            mm = nc.tensor.matmul(hid_ps[:, n % 4], win_s[:, e, a, m * P:(m + 1) * P], xnt[:, a], start=a == 0, stop=a == HALVES - 1)
                        mm.then_inc(hid_made, 1)

                hidden(0)
                pe.wait_ge(gate_done, b + 1)
                for t in range(TILES):
                    mm = nc.tensor.transpose(turn_ps[0:EXPERTS, 1, t * P:(t + 1) * P], gate[:, t], ident[:])
                mm.then_inc(gate_turned, 1)
                hidden(1)
                pe.wait_ge(gate_t_done, b + 1)
                for t in range(TILES):
                    mm = nc.tensor.matmul(y_tile[t], gate_t[:, t * P:(t + 1) * P], bout_s[:], start=True, stop=True, skip_group_check=True)
                mm.then_inc(bias_made, 1)
                for e in range(EXPERTS):
                    pe.wait_ge(hid_done, HALVES * (EXPERTS * b + e + 1))
                    pe.wait_ge(y_used, (EXPERTS + 1) * b + e + 1)
                    for t in range(TILES):
                        for a in range(HALVES):
                            mm = nc.tensor.matmul(y_tile[t], hid[:, e % 2, a, t * P:(t + 1) * P], wout_s[:, e, a], start=a == 0, stop=a == HALVES - 1, skip_group_check=True)
                    mm.then_inc(y_made, 1)
                    if e + 2 < EXPERTS:
                        hidden(e + 2)

        @block.scalar
        def _(act):
            act.wait_ge(weights, 16 * LOADS)
            nc.scalar.activation(gates[:], g_s[:], ACT.Tanh).then_inc(g_tanh, 1)
            with act.Fori(0, BATCH) as b:
                act.wait_ge(stats_done, b + 1)
                nc.scalar.activation(std[:], veps[:], ACT.Sqrt).then_inc(std_done, 1)
                act.wait_ge(best_done, b + 1)
                for t in range(TILES):
                    ins = nc.scalar.activation(prob[:, t], logits[:, t], ACT.Exp, bias=nbest[:, t:t + 1], accum_out=mass[:, t:t + 1])
                ins.then_inc(exp_done, 1)
                for e in range(EXPERTS):
                    for m in range(HALVES):
                        n = e * HALVES + m
                        act.wait_ge(hid_made, HALVES * EXPERTS * b + n + 1)
                        if m == 0:
                            if e >= 2:
                                act.wait_ge(y_made, EXPERTS * b + e - 1)
                            else:
                                act.wait_ge(y_made, EXPERTS * b)
                        nc.scalar.activation(hid[:, e % 2, m], hid_ps[:, n % 4], ACT.Gelu_apprx_tanh, bias=bin_s[:, e, m:m + 1]).then_inc(hid_done, 1)

        @block.vector
        def _(dve):
            V = nc.vector
            dve.wait_ge(weights, 16 * LOADS)
            dve.wait_ge(g_tanh, 1)
            dve.wait_ge(places_made, 1)
            V.tensor_copy(places[:], places_i[:]).then_inc(consts, 1)
            V.tensor_scalar(bo_s[:], bo_s[:], gates[:, 0:1], None, ALU.mult).then_inc(consts, 1)
            dve.wait_ge(consts, 2)
            LINKS = 2 + 1 + 2 + 5 + 1 + 2 + 6

            with dve.Fori(0, BATCH) as b:
                made = [b * LINKS]

                def link(ins):
                    made[0] = made[0] + 1
                    ins.then_inc(chain, 1)
                    dve.wait_ge(chain, made[0])

                dve.wait_ge(o_loaded, 64 * (b + 1))
                link(V.tensor_tensor(osum[:], o_s[:, :, 0], o_s[:, :, 1], ALU.add))
                link(V.tensor_tensor(osum[:], osum[:], o_s[:, :, 2], ALU.add))
                V.tensor_tensor(osum[:], osum[:], o_s[:, :, 3], ALU.add).then_inc(o_summed, 1)
                dve.wait_ge(x_loaded, 16 * (b + 1))
                for t in range(TILES):
                    ins = V.tensor_tensor(x2[:, t], x_s[:, t], bo_s[:], ALU.add)
                link(ins)
                dve.wait_ge(projected, b + 1)
                for t in range(TILES):
                    V.scalar_tensor_tensor(out=x2[:, t], in0=y_tile[t], scalar=gates[:, 0:1], in1=x2[:, t], op0=ALU.mult, op1=ALU.add).then_inc(x2_done, 1)
                dve.wait_ge(x2_done, TILES * (b + 1))
                for t in range(TILES):
                    ins = V.bn_stats(stats[:, t], x2[:, t])
                link(ins)
                dve.sem_inc(passed, 1)
                for t in range(TILES):
                    ins = V.bn_aggr(moments[:, t], stats[:, t])
                link(ins)
                V.tensor_scalar(veps[:], moments[:, :, 1], EPS, None, ALU.add).then_inc(stats_done, 1)
                dve.wait_ge(std_done, b + 1)
                link(V.reciprocal(rstd[:], std[:]))
                link(V.tensor_tensor(fix[:], rstd[:], rstd[:], ALU.mult))
                link(V.tensor_tensor(fix[:], fix[:], veps[:], ALU.mult))
                link(V.tensor_scalar(fix[:], fix[:], -0.5, 1.5, ALU.mult, ALU.add))
                link(V.tensor_tensor(rstd[:], rstd[:], fix[:], ALU.mult))
                for t in range(TILES):
                    V.tensor_scalar(xn[:, t], x2[:, t], moments[:, t, 0:1], rstd[:, t:t + 1], ALU.subtract, ALU.mult).then_inc(normed, 1)
                dve.wait_ge(turned, b + 1)
                for a in range(HALVES):
                    V.tensor_copy(xnt[:, a], turn_ps[:, a]).then_inc(xnt_done, 1)
                dve.wait_ge(routed, b + 1)
                link(V.tensor_copy(logits[:], turn_ps[:, 0, 0:TILES * EXPERTS].rearrange("p (t e) -> p t e", t=TILES)))
                dve.sem_inc(passed, 1)
                for t in range(TILES):
                    ins = V.max(best[:, t], logits[:, t])
                link(ins)
                dve.sem_inc(passed, 1)
                for t in range(TILES):
                    ins = V.max_index(best_i[:, t], best[:, t], logits[:, t])
                link(ins)
                V.tensor_scalar(nbest[:], best[:, :, 0], -1.0, None, ALU.mult).then_inc(best_done, 1)
                link(V.tensor_copy(best_f[:], best_i[:]))
                every = places[:].unsqueeze(1).broadcast_to([P, TILES, EXPERTS])
                link(V.tensor_tensor(pick[:], every, best_f[:, :, 0:1].broadcast_to([P, TILES, EXPERTS]), ALU.is_equal))
                link(V.tensor_tensor(pick2[:], every, best_f[:, :, 1:2].broadcast_to([P, TILES, EXPERTS]), ALU.is_equal))
                link(V.tensor_tensor(pick[:], pick[:], pick2[:], ALU.add))
                dve.wait_ge(exp_done, b + 1)
                link(V.reciprocal(rmass[:], mass[:]))
                link(V.tensor_tensor(pick[:], pick[:], prob[:], ALU.mult))
                V.tensor_tensor(gate[:], pick[:], rmass[:].unsqueeze(2).broadcast_to([P, TILES, EXPERTS]), ALU.mult).then_inc(gate_done, 1)
                dve.wait_ge(gate_turned, b + 1)
                V.tensor_copy(gate_t[:], turn_ps[0:EXPERTS, 1]).then_inc(gate_t_done, 1)
                dve.wait_ge(bias_made, b + 1)
                for t in range(TILES):
                    ins = V.tensor_copy(acc[:, t], y_tile[t])
                ins.then_inc(y_used, 1)
                for e in range(EXPERTS):
                    dve.wait_ge(y_made, EXPERTS * b + e + 1)
                    dve.wait_ge(y_used, (EXPERTS + 1) * b + e + 1)
                    for t in range(TILES):
                        ins = V.scalar_tensor_tensor(out=acc[:, t], in0=y_tile[t], scalar=gate[:, t, e:e + 1], in1=acc[:, t], op0=ALU.mult, op1=ALU.add)
                    ins.then_inc(y_used, 1)
                dve.wait_ge(y_used, (EXPERTS + 1) * (b + 1))
                dve.wait_ge(stored, 16 * b)
                for t in range(TILES):
                    V.scalar_tensor_tensor(out=res[:, t], in0=acc[:, t], scalar=gates[:, 1:2], in1=x2[:, t], op0=ALU.mult, op1=ALU.add).then_inc(finished, 1)


def program(nc, x, ctx_t, ident, g_xattn, g_ffn, wq, bq, wk, bk, wv, bv, wo, bo, router_w, w_in, b_in, w_out, b_out, out):
    q_parts = nc.dram_tensor("q_parts", (3, BATCH * DIM, QUERIES), BF16).ap()
    k_parts = nc.dram_tensor("k_parts", (3, BATCH * DIM, KEYS), BF16).ap()
    v_heads = nc.dram_tensor("v_heads", (BATCH * HEADS, P, KCHUNKS, HEAD_DIM), F32).ap()
    o_parts = nc.dram_tensor("o_parts", (4, BATCH * DIM, QUERIES), F32).ap()
    project_program(nc, x, ctx_t, wq, bq, wk, bk, wv, bv, ident, q_parts, k_parts, v_heads)
    attend_program(nc, q_parts, k_parts, v_heads, ident, o_parts)
    experts_program(nc, x, g_xattn, g_ffn, wo, bo, o_parts, router_w, w_in, b_in, w_out, b_out, ident, out)


_INS = ["x", "ctx_t", "ident", "g_xattn", "g_ffn", "L0_xattn_Wq", "L0_xattn_bq", "L0_xattn_Wk", "L0_xattn_bk",
        "L0_xattn_Wv", "L0_xattn_bv", "L0_xattn_Wo", "L0_xattn_bo", "L0_ffn_router_w", "L0_ffn_w_in", "L0_ffn_b_in",
        "L0_ffn_w_out", "L0_ffn_b_out"]


def kernel(**inputs):
    import numpy as np
    import concourse.bacc as bacc
    from concourse.bass_utils import run_bass_kernel_spmd

    nc = bacc.Bacc("TRN2", target_bir_lowering=False, num_devices=1)
    laid = dict(inputs)
    laid["ctx_t"] = np.transpose(np.asarray(inputs["ctx_1024"]), (0, 2, 1))
    laid["ident"] = np.eye(P, dtype=np.float32)
    arrays, args = {}, []
    for name in _INS:
        a = np.ascontiguousarray(laid[name])
        arrays[f"in_{name}"] = a
        args.append(nc.dram_tensor(f"in_{name}", a.shape, mybir.dt.from_np(a.dtype), kind="ExternalInput").ap())
    out = nc.dram_tensor("out_0", (BATCH, QUERIES, DIM), F32, kind="ExternalOutput").ap()
    program(nc, *args, out)
    r = run_bass_kernel_spmd(nc, [arrays], core_ids=[0])
    return r.results[0]["out_0"]
```

```python
from contextlib import ExitStack

import concourse.bass as bass
from concourse import mybir

F32 = mybir.dt.float32
BF16 = mybir.dt.bfloat16
I32 = mybir.dt.int32
U32 = mybir.dt.uint32
ALU = mybir.AluOpType
ACT = mybir.ActivationFunctionType
AX = mybir.AxisListType

P = 128
BATCH, QUERIES, KEYS, DIM = 16, 512, 1601, 256
HEADS, HEAD_DIM = 16, 16
EXPERTS, HIDDEN = 8, 256
SCALE = HEAD_DIM ** -0.5
EPS = 1e-5
HALVES = DIM // P
TILES = QUERIES // P
KCHUNKS = -(-KEYS // P)
LAST_KEYS = KEYS - (KCHUNKS - 1) * P
BANK = 512
KEY_PIECES = [(c, min(c + BANK, KEYS)) for c in range(0, KEYS, BANK)]

K_PARTS = [0, 1, 2, 0, 1, 0]
Q_PARTS = [0, 0, 0, 1, 1, 2]
GROUPS = len(K_PARTS)
SCORE_ROWS = GROUPS * HEAD_DIM
TAU_ROWS = 3

CHUNKS = 38
RUNS = [(KEYS * c // CHUNKS, KEYS * (c + 1) // CHUNKS) for c in range(CHUNKS)]
CAND = CHUNKS * 8
FIRST, SECOND = 2, 4
ROUNDS = 5
EXACT = 3e-5
GENERAL_STEPS = 26


def project_program(nc, x, ctx_t, wq, bq, wk, bk, wv, bv, ident_in, q_parts, k_parts, v_heads):
    with ExitStack() as ctx:
        def sb(name, shape, dt=F32):
            return ctx.enter_context(nc.sbuf_tensor("p_" + name, shape, dt))

        def sem(name):
            return ctx.enter_context(nc.semaphore("p_" + name))

        RING = 5
        ring = ctx.enter_context(nc.psum_tensor("p_ring", [P, RING, BANK], F32))
        xt = sb("x", [P, 2, TILES, DIM])
        ct = sb("ctx", [P, 2, HALVES, KEYS])
        wq_s, wk_s, wv_s = (sb(n, [P, HALVES, DIM]) for n in ("wq", "wk", "wv"))
        bq_s, bk_s = sb("bq", [P, HALVES]), sb("bk", [P, HALVES])
        bqs = sb("bqs", [P, HALVES])
        bv_s = sb("bv", [P, DIM])
        ident = sb("ident", [P, P])
        stats = sb("stats", [P, TILES, 6])
        moments = sb("moments", [P, TILES, 2])
        std = sb("std", [P, TILES])
        veps = sb("veps", [P, TILES])
        rstd = sb("rstd", [P, TILES])
        fix = sb("fix", [P, TILES])
        xn = sb("xn", [P, TILES, DIM])
        xnt = sb("xnt", [P, HALVES, QUERIES])
        qf = sb("qf", [P, HALVES, QUERIES])
        qr = sb("qr", [P, HALVES, QUERIES])
        qs = sb("qs", [P, 3, HALVES, QUERIES], BF16)
        kf = sb("kf", [P, HALVES, KEYS])
        kr = sb("kr", [P, HALVES, KEYS])
        ks = sb("ks", [P, 3, HALVES, KEYS], BF16)
        vt = sb("v", [P, HEADS, KCHUNKS, HEAD_DIM])

        weights = sem("weights")
        x_loaded = [sem("x_loaded0"), sem("x_loaded1")]
        ctx_loaded = [sem("ctx_loaded0"), sem("ctx_loaded1")]
        stats_done = sem("stats_done")
        std_done = sem("std_done")
        chain = sem("chain")
        normed = sem("normed")
        job_made = sem("job_made")
        job_used = sem("job_used")
        job_used_dve = sem("job_used_dve")
        passed, passed_sp = sem("passed"), sem("passed_sp")
        q_rest = sem("q_rest")
        k_rest = sem("k_rest")
        q_split = sem("q_split")
        k_split = sem("k_split")
        q_high = sem("q_high")
        k_high = sem("k_high")
        q_mid = sem("q_mid")
        k_mid = sem("k_mid")
        q_stored = sem("q_stored")
        k_stored = sem("k_stored")
        v_stored = sem("v_stored")
        consts = sem("consts")

        jobs = [("turn", a) for a in range(HALVES)]
        jobs += [("k", a, c) for a in range(HALVES) for c in range(len(KEY_PIECES))]
        jobs += [("q", a) for a in range(HALVES)]
        jobs += [("v", c) for c in range(KCHUNKS)]
        NJ = len(jobs)
        assert NJ % RING == 0
        by_dve = [j[0] in ("turn", "v") for j in jobs]
        dve_jobs, act_jobs = sum(by_dve), NJ - sum(by_dve)

        def readers_before(b, n):
            return b * dve_jobs + sum(by_dve[:n]), b * act_jobs + n - sum(by_dve[:n])

        block = ctx.enter_context(nc.Block())

        @block.sync
        def _(sp):
            for dst, src in ((wq_s, wq), (wk_s, wk), (wv_s, wv)):
                sp.dma_start(dst[:], src.rearrange("(a p) n -> p a n", p=P)).then_inc(weights, 16)
            for dst, src in ((bq_s, bq), (bk_s, bk)):
                for a in range(HALVES):
                    sp.dma_start(dst[:, a:a + 1], src[a * P:(a + 1) * P].rearrange("(p o) -> p o", o=1)).then_inc(weights, 16)
            sp.dma_start(bv_s[:], bv.rearrange("(o n) -> o n", o=1).broadcast_to([P, DIM])).then_inc(weights, 16)
            sp.dma_start(ident[:], ident_in).then_inc(weights, 16)

            def load(b, u, first):
                if not first:
                    sp.wait_ge(normed, TILES * (b - 1))
                    sp.sem_inc(passed_sp, 1)
                    sp.wait_ge(job_made, NJ * (b - 1))
                    sp.sem_inc(passed_sp, 1)
                sp.dma_start(xt[:, u], x[b].rearrange("(t p) d -> p t d", p=P)).then_inc(x_loaded[u], 16)
                sp.dma_start(ct[:, u], ctx_t[b].rearrange("(a p) n -> p a n", p=P)).then_inc(ctx_loaded[u], 16)

            def store(b):
                sp.wait_ge(q_split, b + 1)
                for s in range(3):
                    sp.dma_start(q_parts[s, bass.ds(b * DIM, DIM)].rearrange("(a p) n -> p a n", p=P), qs[:, s]).then_inc(q_stored, 16)
                sp.wait_ge(k_split, b + 1)
                for s in range(3):
                    sp.dma_start(k_parts[s, bass.ds(b * DIM, DIM)].rearrange("(a p) n -> p a n", p=P), ks[:, s]).then_inc(k_stored, 16)
                sp.wait_ge(job_used_dve, dve_jobs * (b + 1))
                sp.dma_start(v_heads[bass.ds(b * HEADS, HEADS)].rearrange("h p c d -> p h c d")[:, :, 0:KCHUNKS - 1], vt[:, :, 0:KCHUNKS - 1]).then_inc(v_stored, 16)
                sp.dma_start(v_heads[bass.ds(b * HEADS, HEADS)].rearrange("h p c d -> p h c d")[0:LAST_KEYS, :, KCHUNKS - 1:], vt[0:LAST_KEYS, :, KCHUNKS - 1:]).then_inc(v_stored, 16)

            load(0, 0, True)
            load(1, 1, True)
            if BATCH > 2:
                with sp.Fori(0, BATCH // 2 - 1) as g:
                    for u in range(2):
                        load(2 * g + u + 2, u, False)
                        store(2 * g + u)
            for b in range(BATCH - 2, BATCH):
                store(b)
            sp.wait_ge(q_stored, 16 * 3 * BATCH)
            sp.wait_ge(k_stored, 16 * 3 * BATCH)
            sp.wait_ge(v_stored, 16 * 2 * BATCH)

        @block.tensor
        def _(pe):
            pe.wait_ge(weights, 16 * 9)
            def pair(g):
                for u in range(2):
                    b = 2 * g + u
                    pe.wait_ge(normed, TILES * (b + 1))
                    for n, job in enumerate(jobs):
                        bank = ring[:, n % RING]
                        if n >= RING:
                            by, m = by_dve[n - RING], n - RING
                            d, a = readers_before(b, m + 1)
                            pe.wait_ge(job_used_dve if by else job_used, d if by else a)
                        elif not isinstance(b, int) or b > 0:
                            m = NJ + n - RING
                            by = by_dve[m]
                            d, a = readers_before(b, m + 1)
                            with_prev = (d - dve_jobs) if by else (a - act_jobs)
                            pe.wait_ge(job_used_dve if by else job_used, with_prev)
                        if job[0] == "turn":
                            a = job[1]
                            for t in range(TILES):
                                mm = nc.tensor.transpose(bank[:, t * P:(t + 1) * P], xn[:, t, a * P:(a + 1) * P], ident[:])
                        elif job[0] == "q":
                            if job[1] == 0:
                                pe.wait_ge(job_used_dve, b * dve_jobs + HALVES)
                            for c in range(HALVES):
                                mm = nc.tensor.matmul(bank, wq_s[:, c, job[1] * P:(job[1] + 1) * P], xnt[:, c], start=c == 0, stop=c == HALVES - 1)
                        elif job[0] == "k":
                            if job[1:] == (0, 0):
                                pe.wait_ge(ctx_loaded[u], 16 * (g + 1))
                            lo, hi = KEY_PIECES[job[2]]
                            for c in range(HALVES):
                                mm = nc.tensor.matmul(bank[:, 0:hi - lo], wk_s[:, c, job[1] * P:(job[1] + 1) * P], ct[:, u, c, lo:hi], start=c == 0, stop=c == HALVES - 1)
                        else:
                            lo, hi = job[1] * P, min(job[1] * P + P, KEYS)
                            for c in range(HALVES):
                                mm = nc.tensor.matmul(bank[0:hi - lo, 0:DIM], ct[:, u, c, lo:hi], wv_s[:, c], start=c == 0, stop=c == HALVES - 1)
                        mm.then_inc(job_made, 1)

            pair(0)
            with pe.Fori(1, BATCH // 2) as g:
                pair(g)

        @block.scalar
        def _(act):
            act.wait_ge(weights, 16 * 9)
            nc.scalar.mul(bqs[:], bq_s[:], SCALE).then_inc(consts, 1)
            act.wait_ge(consts, 1)
            def root(b):
                act.wait_ge(stats_done, b + 1)
                nc.scalar.activation(std[:], veps[:], ACT.Sqrt).then_inc(std_done, 1)

            def batch(b, last=False):
                for n, job in enumerate(jobs):
                    if job[0] == "k":
                        a, c = job[1:]
                        if (a, c) == (0, 0):
                            act.wait_ge(k_rest, b)
                        lo, hi = KEY_PIECES[c]
                        act.wait_ge(job_made, NJ * b + n + 1)
                        nc.scalar.activation(kf[:, a, lo:hi], ring[:, n % RING, 0:hi - lo], ACT.Identity, bias=bk_s[:, a:a + 1]).then_inc(job_used, 1)
                        if (a, c) == (HALVES - 1, len(KEY_PIECES) - 1):
                            if not last:
                                root(b + 1)
                            act.wait_ge(job_used, readers_before(b, n + 1)[1])
                            act.wait_ge(k_stored, 48 * b)
                            nc.scalar.copy(ks[:, 0], kf[:]).then_inc(k_high, 1)
                    elif job[0] == "q":
                        a = job[1]
                        if a == 0:
                            act.wait_ge(q_rest, b)
                        act.wait_ge(job_made, NJ * b + n + 1)
                        nc.scalar.activation(qf[:, a], ring[:, n % RING], ACT.Identity, bias=bqs[:, a:a + 1], scale=SCALE).then_inc(job_used, 1)
                        if a == HALVES - 1:
                            act.wait_ge(job_used, readers_before(b, n + 1)[1])
                            act.wait_ge(q_stored, 48 * b)
                            nc.scalar.copy(qs[:, 0], qf[:]).then_inc(q_high, 1)

            root(0)
            with act.Fori(0, BATCH - 1) as b:
                batch(b)
            batch(BATCH - 1, last=True)

        @block.gpsimd
        def _(pool):
            with pool.Fori(0, BATCH) as b:
                pool.wait_ge(k_high, b + 1)
                pool.wait_ge(k_split, b)
                nc.gpsimd.tensor_tensor(kr[:], kf[:], ks[:, 0], ALU.subtract).then_inc(k_rest, 1)
                pool.wait_ge(q_high, b + 1)
                pool.wait_ge(q_split, b)
                nc.gpsimd.tensor_tensor(qr[:], qf[:], qs[:, 0], ALU.subtract).then_inc(q_rest, 1)

        @block.vector
        def _(dve):
            dve.wait_ge(weights, 16 * 9)
            LINKS = 5 + 2

            def norm(b, u, n_loaded):
                made = [LINKS * b]

                def link(ins):
                    made[0] = made[0] + 1
                    ins.then_inc(chain, 1)
                    dve.wait_ge(chain, made[0])

                dve.wait_ge(x_loaded[u], 16 * n_loaded)
                for t in range(TILES):
                    ins = nc.vector.bn_stats(stats[:, t], xt[:, u, t])
                link(ins)
                dve.sem_inc(passed, 1)
                for t in range(TILES):
                    ins = nc.vector.bn_aggr(moments[:, t], stats[:, t])
                link(ins)
                nc.vector.tensor_scalar(veps[:], moments[:, :, 1], EPS, None, ALU.add).then_inc(stats_done, 1)
                dve.wait_ge(std_done, b + 1)
                link(nc.vector.reciprocal(rstd[:], std[:]))
                link(nc.vector.tensor_tensor(fix[:], rstd[:], rstd[:], ALU.mult))
                link(nc.vector.tensor_tensor(fix[:], fix[:], veps[:], ALU.mult))
                link(nc.vector.tensor_scalar(fix[:], fix[:], -0.5, 1.5, ALU.mult, ALU.add))
                link(nc.vector.tensor_tensor(rstd[:], rstd[:], fix[:], ALU.mult))
                for t in range(TILES):
                    nc.vector.tensor_scalar(xn[:, t], xt[:, u, t], moments[:, t, 0:1], rstd[:, t:t + 1], ALU.subtract, ALU.mult).then_inc(normed, 1)

            def batch(b, u, g, last=False):
                for n, job in enumerate(jobs):
                    if job[0] == "turn":
                        if job[1] == 0:
                            dve.wait_ge(q_high, b)
                        dve.wait_ge(job_made, NJ * b + n + 1)
                        nc.vector.tensor_copy(xnt[:, job[1]], ring[:, n % RING]).then_inc(job_used_dve, 1)
                if not last:
                    norm(b + 1, 1 - u, g + 1 + u)
                for n, job in enumerate(jobs):
                    if job[0] == "v":
                        c = job[1]
                        rows = P if c < KCHUNKS - 1 else LAST_KEYS
                        if c == 0:
                            dve.wait_ge(v_stored, 32 * b)
                        dve.wait_ge(job_made, NJ * b + n + 1)
                        nc.vector.tensor_tensor(vt[0:rows, :, c, :], ring[0:rows, n % RING, 0:DIM].rearrange("p (h d) -> p h d", h=HEADS),
                                                bv_s[0:rows].rearrange("p (h d) -> p h d", h=HEADS), ALU.add).then_inc(job_used_dve, 1)
                for rest, high, mid, split, r, s in ((q_rest, q_high, q_mid, q_split, qr, qs), (k_rest, k_high, k_mid, k_split, kr, ks)):
                    dve.wait_ge(rest, b + 1)
                    nc.vector.tensor_copy(s[:, 1], r[:]).then_inc(mid, 1)
                    dve.wait_ge(mid, b + 1)
                    nc.vector.tensor_tensor(s[:, 2], r[:], s[:, 1], ALU.subtract).then_inc(split, 1)

            norm(0, 0, 1)
            with dve.Fori(0, BATCH // 2 - 1) as g:
                for u in range(2):
                    batch(2 * g + u, u, g)
            for u in range(2):
                batch(BATCH - 2 + u, u, BATCH // 2 - 1, last=u == 1)


def attend_program(nc, q_parts, k_parts, v_heads, ident_in, o_parts):
    N = BATCH * HEADS
    U = 6
    SLOTS = 3
    RING = 3
    LAG = 3
    S_PIECES = [(t, lo, min(lo + 2 * BANK, KEYS)) for t in range(TILES) for lo in range(0, KEYS, 2 * BANK)]
    T_PIECES = [range(c, min(c + 2, KCHUNKS)) for c in range(0, KCHUNKS, 2)]
    NS, NT = len(S_PIECES), len(T_PIECES)
    assert (NS + NT) % RING == 0 and U % SLOTS == 0 and U % 2 == 0

    def groups(do_s, do_t):
        place, out = 0, []
        for g in range(TILES):
            own = []
            for kind, n, there in [("s", 2 * g, do_s), ("s", 2 * g + 1, do_s)] + [("t", k, do_t) for k in range(2 * g, min(2 * g + 2, NT))]:
                if there:
                    own.append((kind, n, place))
                    place += 1
            out.append(own)
        return out

    def before(i):
        if isinstance(i, int):
            return NS * min(i, N) + NT * min(max(0, i - LAG), N)
        return i * (NS + NT) - NT * LAG

    def slot(i, place):
        return ((before(i) if isinstance(i, int) else -NT * LAG) + place) % RING

    def score_place(n, do_t):
        return next(p for own in groups(True, do_t) for kind, m, p in own if kind == "s" and m == n)

    def walk(engine, step):
        for i in range(U):
            step(i, i)
        with engine.Fori(1, N // U) as g:
            for u in range(U):
                step(g * U + u, u)
        for i in range(N // U * U, N + LAG + 1):
            step(i, i % U)

    def has(i, lag):
        return not isinstance(i, int) or 0 <= i - lag < N

    with ExitStack() as ctx:
        def sb(name, shape, dt=F32):
            return ctx.enter_context(nc.sbuf_tensor("a_" + name, shape, dt))

        def sem(name):
            return ctx.enter_context(nc.semaphore("a_" + name))

        ring = ctx.enter_context(nc.psum_tensor("a_ring", [P, RING, 2 * BANK], F32))
        out_ps = ctx.enter_context(nc.psum_tensor("a_out", [P, BANK], F32))
        turn_ps = ctx.enter_context(nc.psum_tensor("a_turn", [P, BANK], F32))

        k_st = sb("k", [P, U, KEYS], BF16)
        q_st = sb("q", [P, U, QUERIES], BF16)
        v_st = sb("v", [P, U, KCHUNKS, HEAD_DIM])
        scores = sb("scores", [P, SLOTS, TILES, KEYS])
        attn = sb("attn", [P, NT, 2 * BANK])
        o_sb = sb("o", [P, 2, QUERIES])
        cand = sb("cand", [P, SLOTS, TILES, CHUNKS, 8])
        junk, junk2 = sb("junk", [P, KEYS]), sb("junk2", [P, KEYS])
        junk_act = sb("junk_act", [P, TILES, CAND])
        junk_act0 = sb("junk_act0", [P, TILES, CHUNKS * SECOND])
        zeros = sb("zeros", [P, 1])
        ident_f = sb("ident_f", [P, P])
        ident = sb("ident", [P, P], BF16)
        ones = sb("ones", [P, 1], BF16)
        ntau = sb("ntau", [P, 2, TILES])
        ntop = sb("ntop", [P, 2, TILES])
        excess = sb("excess", [P, 2, ROUNDS, TILES])
        own_excess = sb("own_excess", [P, TILES])
        count = sb("count", [P, TILES])
        model = sb("model", [P, TILES])
        inv = sb("inv", [P, 2, TILES])
        move = sb("move", [P, 2, TILES])
        w1, w2, w3 = (sb(n, [P, TILES]) for n in ("w1", "w2", "w3"))
        per_count = sb("per_count", [P, TILES])
        e_plus1, e_bound = sb("e_plus1", [P, TILES]), sb("e_bound", [P, TILES])
        square = sb("square", [P, TILES])
        fall = sb("fall", [P, TILES])
        miss = sb("miss", [P, TILES])
        unit = sb("unit", [P, TILES])
        bad = sb("bad", [P, TILES], BF16)
        weigh = sb("weigh", [P, TILES])
        tile_bits = sb("tile_bits", [1, TILES])
        bit_sum = sb("bit_sum", [1, 1])
        bad_bits = sb("bad_bits", [1, 1], I32)
        g_excess, g_count, g_over1, g_miss, g_move = (sb(n, [P, 1]) for n in ("g_excess", "g_count", "g_over1", "g_miss", "g_move"))
        over1 = sb("over1", [P, TILES])
        rest = sb("rest", [P, TILES])
        split = sb("split", [P, TILES, TAU_ROWS], BF16)
        flag = sb("flag", [P, 32])
        flag_t = sb("flag_t", [P, 32])
        flag_row = sb("flag_row", [1, 4, 32])
        flag_i = sb("flag_i", [1, 1], I32)

        loaded = [sem(f"loaded{u}") for u in range(U)]
        ident_loaded = sem("ident_loaded")
        setup = sem("setup")
        piece_made = sem("piece_made")
        piece_used = sem("piece_used")
        products = sem("products")
        out_copied = sem("out_copied")
        out_stored = [sem("out_stored0"), sem("out_stored1")]
        cand_made = sem("cand_made")
        tau_tried = sem("tau_tried")
        tau_tried_last = sem("tau_tried_last")
        model_made = sem("model_made")
        fall_made = sem("fall_made")
        inv_made = sem("inv_made")
        stepped = sem("stepped")
        excess_made = sem("excess_made")
        bad_ready = sem("bad_ready")
        bad_counted = sem("bad_counted")
        settled = sem("settled")
        tau_split = sem("tau_split")
        pool_chain = sem("pool_chain")
        tau_turned = sem("tau_turned")
        tau_in_q = sem("tau_in_q")
        chain = sem("chain")
        passed, passed_pool = sem("passed"), sem("passed_pool")
        general = sem("general")
        SETUP = 6 + TILES
        FIRST_ROUNDS = 3
        LOADS = len(K_PARTS) + len(Q_PARTS) + 2

        block = ctx.enter_context(nc.Block())

        @block.sync
        def _(sp):
            sp.dma_start(ident_f[:], ident_in).then_inc(ident_loaded, 16)

            def load(i, u):
                for parts, st, run in ((K_PARTS, k_st, k_parts), (Q_PARTS, q_st, q_parts)):
                    for n, s in enumerate(parts):
                        sp.dma_start(st[n * HEAD_DIM:(n + 1) * HEAD_DIM, u], run[s, bass.ds(i * HEAD_DIM, HEAD_DIM)]).then_inc(loaded[u], 16)
                sp.dma_start(v_st[:, u, 0:KCHUNKS - 1], v_heads[i][:, 0:KCHUNKS - 1]).then_inc(loaded[u], 16)
                sp.dma_start(v_st[0:LAST_KEYS, u, KCHUNKS - 1:], v_heads[i][0:LAST_KEYS, KCHUNKS - 1:]).then_inc(loaded[u], 16)

            def store(i, u):
                sp.wait_ge(out_copied, i + 1)
                for s in range(4):
                    sp.dma_start(o_parts[s, bass.ds(i * HEAD_DIM, HEAD_DIM)], o_sb[32 * s:32 * s + HEAD_DIM, u % 2]).then_inc(out_stored[u % 2], 16)

            for i in range(U):
                load(i, i)
            with sp.Fori(0, N // U - 1) as g:
                for u in range(U):
                    i = g * U + u
                    store(i, u)
                    sp.wait_ge(products, NT * (i + 1))
                    load(i + U, u)
            for i in range((N // U - 1) * U, N):
                if i + U < N:
                    sp.wait_ge(products, NT * (i + 1))
                    load(i + U, i % U)
                store(i, i % U)
            for slot_stored in out_stored:
                sp.wait_ge(slot_stored, 64 * N // 2)

        @block.tensor
        def _(pe):
            pe.wait_ge(setup, SETUP)

            def multiply(i, k, u, t_place):
                pe.wait_ge(piece_used, t_place + 1)
                if k == 0:
                    pe.wait_ge(out_copied, i)
                for c in T_PIECES[k]:
                    rows = P if c < KCHUNKS - 1 else LAST_KEYS
                    at = 32 * (c % 4)
                    mm = nc.tensor.matmul(out_ps[at:at + HEAD_DIM], v_st[0:rows, u, c], attn[0:rows, k, (c % 2) * BANK:(c % 2 + 1) * BANK],
                                          start=c < 4, stop=c >= KCHUNKS - 4)
                mm.then_inc(products, 1)

            def before_prev(i):
                return before(i - 1) if isinstance(i, int) else before(i) - NS - NT

            def count_bad(i):
                pe.wait_ge(bad_ready, i + 1)
                nc.tensor.matmul(turn_ps[0:1, 0:TILES], ones[:], bad[:], start=True, stop=True).then_inc(bad_counted, 1)

            def turn_tau(i):
                pe.wait_ge(tau_split, i + 1)
                if not isinstance(i, int) or i >= 1:
                    pe.wait_ge(tau_in_q, i)
                for t in range(TILES):
                    mm = nc.tensor.matmul(turn_ps[SCORE_ROWS:SCORE_ROWS + TAU_ROWS, t * P:(t + 1) * P], split[:, t], ident[:], start=True, stop=True)
                mm.then_inc(tau_turned, 1)

            def step(i, u, g):
                do_s, do_t = has(i, 0), has(i, LAG)
                ut = (u - LAG) % U
                if do_s:
                    pe.wait_ge(loaded[u], 16 * LOADS * (g + 1))
                order = groups(do_s, do_t)
                turn_at = ("s", 1) if do_s else ("t", 0)
                for part, own in enumerate(order):
                    for kind, n, place in own:
                        if (kind, n) == turn_at and do_t:
                            turn_tau(i - LAG)
                        if (kind, n) == ("t", 0):
                            pe.wait_ge(tau_in_q, i - LAG + 1)
                        seq = before(i) + place
                        if not isinstance(i, int) or seq >= RING:
                            pe.wait_ge(piece_used, seq - RING + 1)
                        at = ring[:, slot(i, place)]
                        if kind == "s":
                            t, lo, hi = S_PIECES[n]
                            for c in range(lo, hi, BANK):
                                w = min(BANK, hi - c)
                                mm = nc.tensor.matmul(at[:, c - lo:c - lo + w], q_st[0:SCORE_ROWS, u, t * P:(t + 1) * P], k_st[0:SCORE_ROWS, u, c:c + w], start=True, stop=True)
                        else:
                            for m, c in enumerate(T_PIECES[n]):
                                rows = P if c < KCHUNKS - 1 else LAST_KEYS
                                mm = nc.tensor.matmul(at[0:rows, m * BANK:(m + 1) * BANK], k_st[0:SCORE_ROWS + TAU_ROWS, ut, c * P:c * P + rows],
                                                      q_st[0:SCORE_ROWS + TAU_ROWS, ut], start=True, stop=True)
                        mm.then_inc(piece_made, 1)
                    if part == 0:
                        if has(i, LAG + 1):
                            last = NT - 1
                            p = next(p for o in groups(has(i, 1), has(i, LAG + 1)) for kd, n, p in o if (kd, n) == ("t", last))
                            multiply(i - LAG - 1, last, (ut - 1) % U, before_prev(i) + p)
                    else:
                        for kd, n, p in order[part - 1]:
                            if kd == "t":
                                multiply(i - LAG, n, ut, before(i) + p)
                    if part == 2 and has(i, 2):
                        count_bad(i - 2)
            for i in range(U):
                step(i, i, 0)
            with pe.Fori(1, N // U) as g:
                for u in range(U):
                    step(g * U + u, u, g)
            for i in range(N // U * U, N + LAG + 1):
                step(i, i % U, i // U)

        @block.scalar
        def _(act):
            act.wait_ge(setup, SETUP)

            def measure_excess(i, u, r):
                if r < FIRST_ROUNDS:
                    act.wait_ge(tau_tried, FIRST_ROUNDS * i + r + 1)
                else:
                    act.wait_ge(tau_tried_last, (ROUNDS - FIRST_ROUNDS) * i + r - FIRST_ROUNDS + 1)
                for t in range(TILES):
                    w, into = (SECOND, junk_act0) if r == 0 else (8, junk_act)
                    ins = nc.scalar.activation(into[:, t].rearrange("p (a b) -> p a b", a=CHUNKS), cand[:, u % SLOTS, t, :, 0:w], ACT.Relu,
                                               bias=ntau[:, u % 2, t:t + 1], accum_out=excess[:, u % 2, r, t:t + 1])
                ins.then_inc(excess_made, 1)

            def step(i, u):
                do_s, do_t = has(i, 0), has(i, LAG)
                ut = (u - LAG) % U
                if do_s and (not isinstance(i, int) or i >= SLOTS):
                    act.wait_ge(settled, i - SLOTS + 1)
                turn_at = ("s", 1) if do_s else ("t", 0)
                for g, own in enumerate(groups(do_s, do_t)):
                    for kind, n, place in own:
                        seq = before(i) + place
                        at = ring[:, slot(i, place)]
                        if (kind, n) == turn_at and do_t:
                            act.wait_ge(tau_turned, i - LAG + 1)
                            nc.scalar.copy(q_st[SCORE_ROWS:SCORE_ROWS + TAU_ROWS, ut], turn_ps[SCORE_ROWS:SCORE_ROWS + TAU_ROWS]).then_inc(tau_in_q, 1)
                        if kind == "t" and (not isinstance(i, int) or i > LAG):
                            act.wait_ge(products, NT * (i - LAG - 1) + n + 1)
                        act.wait_ge(piece_made, seq + 1)
                        if kind == "s":
                            t, lo, hi = S_PIECES[n]
                            nc.scalar.copy(scores[:, u % SLOTS, t, lo:hi], at[:, 0:hi - lo]).then_inc(piece_used, 1)
                        else:
                            rows = P if T_PIECES[n][-1] < KCHUNKS - 1 else LAST_KEYS
                            w = len(T_PIECES[n]) * BANK
                            nc.scalar.activation(attn[0:rows, n, 0:w], at[0:rows, 0:w], ACT.Relu).then_inc(piece_used, 1)
                    if g == 0 and has(i, LAG + 1):
                        o_slot = (u - LAG - 1) % 2
                        act.wait_ge(products, NT * (i - LAG))
                        if not isinstance(i, int) or i > LAG + 2:
                            act.wait_ge(out_stored[o_slot], 32 * (i - LAG - 1 - o_slot))
                        nc.scalar.copy(o_sb[:, o_slot], out_ps[:]).then_inc(out_copied, 1)
                    if g < 2 and has(i, 2):
                        measure_excess(i - 2, (u - 2) % U, FIRST_ROUNDS + g)
                    if g > 0 and has(i, 1):
                        measure_excess(i - 1, (u - 1) % U, g - 1)

            walk(act, step)

        @block.vector
        def _(dve):
            nc.vector.memset(k_st[SCORE_ROWS:SCORE_ROWS + TAU_ROWS], 1.0).then_inc(setup, 1)
            nc.vector.memset(ones[:], 1.0).then_inc(setup, 1)
            nc.vector.memset(zeros[:], 0.0).then_inc(setup, 1)
            nc.vector.memset(unit[:], 1.0).then_inc(setup, 1)
            for t in range(TILES):
                nc.vector.memset(weigh[:, t:t + 1], 2.0 ** t).then_inc(setup, 1)
            nc.vector.memset(out_ps[:], 0.0).then_inc(setup, 1)
            nc.vector.memset(flag[:], 0.0).then_inc(chain, 1)
            dve.wait_ge(ident_loaded, 16)
            nc.vector.tensor_copy(ident[:], ident_f[:]).then_inc(setup, 1)
            dve.wait_ge(setup, SETUP)
            dve.wait_ge(chain, 1)
            unsettled = dve.alloc_register("unsettled")
            bits = dve.alloc_register("bits")
            steps_left = dve.alloc_register("steps_left")
            V = nc.vector

            def view(tile, values, width, n):
                flat = tile[:, n * width:(n + 1) * width]
                return flat.rearrange("p (a b) -> p a b", a=CHUNKS) if len(values.shape) == 3 else flat

            def zeros_like(values):
                return (zeros[:].unsqueeze(2) if len(values.shape) == 3 else zeros[:]).broadcast_to(list(values.shape))

            def measure_own(t, values, width, nt):
                return V.scalar_tensor_tensor(out=view(junk, values, width, TILES + t), in0=values, scalar=nt[:, t:t + 1], in1=zeros_like(values), op0=ALU.add, op1=ALU.max,
                                              accum_out=own_excess[:, t:t + 1])

            def measure_count(t, values, width, nt):
                return V.scalar_tensor_tensor(out=view(junk, values, width, t), in0=values, scalar=nt[:, t:t + 1], in1=zeros_like(values), op0=ALU.add, op1=ALU.is_gt,
                                              accum_out=count[:, t:t + 1])


            def guess(link, e, nt, recip):
                V.scalar_tensor_tensor(out=w2[:], in0=e, scalar=1.0, in1=e, op0=ALU.subtract, op1=ALU.mult)
                yield from link(V.tensor_scalar(w1[:], e, 1.0, None, ALU.add))
                yield from link(V.scalar_tensor_tensor(out=w1[:], in0=count[:], scalar=1.0, in1=w1[:], op0=ALU.max, op1=ALU.mult))
                yield from link(V.reciprocal(recip, w1[:]))
                yield from link(V.scalar_tensor_tensor(out=w3[:], in0=w2[:], scalar=-2.0, in1=recip, op0=ALU.mult, op1=ALU.mult))
                yield from link(V.tensor_tensor(nt, nt, w3[:], ALU.add))

            def start(i, u, link):
                c, nt = cand[:, u % SLOTS], ntau[:, u % 2]
                if not isinstance(i, int) or i >= 2:
                    dve.wait_ge(tau_split, i - 1)
                    dve.sem_inc(passed, 1)
                V.tensor_reduce(ntop[:, u % 2], c[:, :, :, 0], AX.X, ALU.max, negate=True)
                yield from link(V.tensor_reduce(w1[:], c[:, :, :, 0], AX.X, ALU.add))
                yield from link(V.tensor_scalar(nt, w1[:], -1.0 / CHUNKS, None, ALU.mult))
                for t in range(TILES):
                    measure_own(t, c[:, t, :, 0:FIRST], CHUNKS * FIRST, nt)
                    ins = measure_count(t, c[:, t, :, 0:FIRST], CHUNKS * FIRST, nt)
                yield from link(ins)
                yield from guess(link, own_excess[:], nt, w1[:])
                for t in range(TILES):
                    ins = measure_count(t, c[:, t, :, 0:SECOND], CHUNKS * SECOND, nt)
                ins.then_inc(tau_tried, 1)
                dve.wait_ge(tau_tried, FIRST_ROUNDS * i + 1)

            def second(i, u, link):
                e, nt = excess[:, u % 2, 0], ntau[:, u % 2]
                dve.wait_ge(excess_made, ROUNDS * i + 1)
                yield from guess(link, e, nt, per_count[:])
                yield from link(V.scalar_tensor_tensor(out=nt, in0=ntop[:, u % 2], scalar=1.0, in1=nt, op0=ALU.add, op1=ALU.min))
                V.scalar_tensor_tensor(out=nt, in0=ntop[:, u % 2], scalar=1.0 / KEYS, in1=nt, op0=ALU.add, op1=ALU.max).then_inc(tau_tried, 1)
                dve.wait_ge(tau_tried, FIRST_ROUNDS * i + 2)

            def third(i, u, link):
                e, nt, mv = excess[:, u % 2, 1], ntau[:, u % 2], move[:, u % 2]
                dve.wait_ge(excess_made, ROUNDS * i + 2)
                dve.sem_inc(passed, 1)
                dve.wait_ge(model_made, i + 1)
                yield from link(V.tensor_scalar(w1[:], e, 1.0, None, ALU.add))
                yield from link(V.reciprocal(w1[:], w1[:]))
                yield from link(V.scalar_tensor_tensor(out=w2[:], in0=e, scalar=1.0, in1=model[:], op0=ALU.subtract, op1=ALU.mult))
                yield from link(V.scalar_tensor_tensor(out=mv, in0=w2[:], scalar=2.0, in1=w1[:], op0=ALU.mult, op1=ALU.mult))
                V.tensor_tensor(nt, nt, mv, ALU.subtract).then_inc(tau_tried, 1)
                dve.wait_ge(tau_tried, FIRST_ROUNDS * i + 3)

            def slope(i, u, link):
                iv = inv[:, u % 2]
                dve.wait_ge(fall_made, i + 1)
                yield from link(V.tensor_scalar(w1[:], fall[:], 1e-30, None, ALU.max))
                yield from link(V.reciprocal(w1[:], w1[:]))
                yield from link(V.tensor_tensor(w1[:], w1[:], square[:], ALU.mult))
                yield from link(V.scalar_tensor_tensor(out=w1[:], in0=model[:], scalar=0.5, in1=w1[:], op0=ALU.mult, op1=ALU.max))
                V.scalar_tensor_tensor(out=iv, in0=model[:], scalar=2.0, in1=w1[:], op0=ALU.mult, op1=ALU.min).then_inc(inv_made, 1)
                dve.wait_ge(inv_made, i + 1)

            def judge(i, u, link):
                yield from link(V.tensor_reduce(w1[:], cand[:, u % SLOTS, :, :, 7], AX.X, ALU.max))
                dve.wait_ge(stepped, i + 1)
                yield from link(V.tensor_tensor(w1[:], w1[:], ntau[:, u % 2], ALU.add))
                yield from link(V.tensor_scalar(w1[:], w1[:], 0.0, None, ALU.is_gt))
                V.scalar_tensor_tensor(out=bad[:], in0=miss[:], scalar=EXACT ** 2, in1=w1[:], op0=ALU.is_gt, op1=ALU.max).then_inc(bad_ready, 1)
                dve.wait_ge(bad_ready, i + 1)

            FIRST_LINKS = (2 + 1 + 5) + (5 + 1) + 4 + 4
            LAST_LINKS = 3 + 2

            def links_before(i):
                if isinstance(i, int):
                    return 1 + FIRST_LINKS * min(max(0, i - 1), N) + LAST_LINKS * min(max(0, i - 2), N)
                return i * (FIRST_LINKS + LAST_LINKS) + (1 - FIRST_LINKS - 2 * LAST_LINKS)

            def general_path(sc, nt, lead, iv):
                dve.sem_clear(general)
                links = [0]

                def link(ins):
                    links[0] += 1
                    ins.then_inc(general, 1)
                    dve.wait_ge(general, links[0])

                def mark(ins):
                    links[0] += 1
                    ins.then_inc(general, 1)

                every = zeros[:].broadcast_to([P, KEYS])
                measured = V.scalar_tensor_tensor(out=junk[:], in0=sc, scalar=nt, in1=every, op0=ALU.add, op1=ALU.max, accum_out=g_excess[:])
                if iv is None:
                    mark(measured)
                    link(V.scalar_tensor_tensor(out=junk2[:], in0=sc, scalar=nt, in1=every, op0=ALU.add, op1=ALU.is_gt, accum_out=g_count[:]))
                    link(V.tensor_scalar(g_count[:], g_count[:], 1.0, None, ALU.max))
                    mark(V.reciprocal(g_count[:], g_count[:]))
                    iv = g_count[:]
                else:
                    link(measured)
                link(V.tensor_scalar(g_over1[:], g_excess[:], 1.0, None, ALU.subtract))
                mark(V.tensor_tensor(g_miss[:], g_over1[:], g_over1[:], ALU.mult))
                link(V.tensor_tensor(g_move[:], g_over1[:], iv, ALU.mult))
                link(V.tensor_scalar(flag[:, 0:1], g_miss[:], EXACT ** 2, None, ALU.is_gt))
                link(V.tensor_tensor(nt, nt, g_move[:], ALU.subtract))
                mark(V.scalar_tensor_tensor(out=nt, in0=lead, scalar=1.0, in1=nt, op0=ALU.add, op1=ALU.min))
                link(V.transpose(flag_t[:], flag[:]))
                mark(V.scalar_tensor_tensor(out=nt, in0=lead, scalar=1.0 / KEYS, in1=nt, op0=ALU.add, op1=ALU.max))
                for q in range(P // 32):
                    ins = V.tensor_copy(flag_row[:, q], flag_t[32 * q:32 * q + 1])
                link(ins)
                with nc.allow_low_precision(reason="counts up to 128 are exact as integers"):
                    link(V.tensor_reduce(flag_i[:], flag_row[:], AX.XY, ALU.add))
                dve.reg_load(unsettled, flag_i[:])
                dve.reg_sub(steps_left, steps_left, 1)
                dve.reg_mul(unsettled, unsettled, steps_left)

            def settle(i, u, link):
                dve.wait_ge(bad_counted, i + 1)
                yield from link(V.scalar_tensor_tensor(out=tile_bits[:], in0=turn_ps[0:1, 0:TILES], scalar=1.0, in1=weigh[0:1], op0=ALU.min, op1=ALU.mult, accum_out=bit_sum[:]))
                yield from link(V.tensor_copy(bad_bits[:], bit_sum[:]))
                dve.sem_inc(passed, 1)
                yield
                yield
                dve.reg_load(bits, bad_bits[:])
                with dve.If(dve.snap(bits) > 0):
                    for t in range(TILES):
                        dve.reg_alu(unsettled, bits, 1 << t, ALU.bitwise_and)
                        with dve.If(dve.snap(unsettled) > 0):
                            sc, nt, lead = scores[:, u % SLOTS, t], ntau[:, u % 2, t:t + 1], ntop[:, u % 2, t:t + 1]
                            dve.reg_mov(steps_left, GENERAL_STEPS + 1)
                            general_path(sc, nt, lead, inv[:, u % 2, t:t + 1])
                            with dve.While(lambda: dve.snap(unsettled) > 0):
                                general_path(sc, nt, lead, None)
                dve.sem_inc(settled, 1)

            def step(i, u):
                made = [links_before(i)]

                def link(ins):
                    made[0] = made[0] + 1
                    ins.then_inc(chain, 1)
                    own = made[0]
                    yield
                    dve.wait_ge(chain, own)

                def beside(t):
                    last, prev = (u - 2) % U, (u - 1) % U
                    if t == 0 and has(i, 1):
                        dve.wait_ge(cand_made, i)
                        yield from start(i - 1, prev, link)
                    if t == 1:
                        yield
                        yield
                        yield
                    if t == 1 and has(i, 1):
                        yield from second(i - 1, prev, link)
                    if t == 1 and has(i, 2):
                        yield from judge(i - 2, last, link)
                    if t == 2 and has(i, 1):
                        yield from third(i - 1, prev, link)
                    if t == 2 and has(i, 2):
                        yield from settle(i - 2, last, link)
                    if t == 3 and has(i, 1):
                        yield from slope(i - 1, prev, link)
                    dve.sem_inc(passed, 1)

                for t in range(TILES):
                    side = beside(t)
                    if has(i, 0):
                        dve.wait_ge(piece_used, before(i) + score_place(2 * t + 1, has(i, LAG)) + 1)
                        dve.sem_inc(passed, 1)
                        for c, (lo, hi) in enumerate(RUNS):
                            ins = V.max(cand[:, u % SLOTS, t, c], scores[:, u % SLOTS, t, lo:hi])
                            if c % 2:
                                next(side, None)
                        if t == TILES - 1:
                            ins.then_inc(cand_made, 1)
                    for _ in side:
                        pass

            walk(dve, step)

        @block.gpsimd
        def _(pool):
            pool.wait_ge(setup, SETUP)
            G = nc.gpsimd
            FIRST_LINKS, LAST_LINKS = 3 + 1 + 2, 2 + 3 + 3

            def links_before(i):
                if isinstance(i, int):
                    return FIRST_LINKS * min(max(0, i - 1), N) + LAST_LINKS * min(max(0, i - 2), N)
                return i * (FIRST_LINKS + LAST_LINKS) - FIRST_LINKS - 2 * LAST_LINKS

            def step(i, u):
                made = [links_before(i)]

                def link(ins):
                    made[0] = made[0] + 1
                    ins.then_inc(pool_chain, 1)
                    pool.wait_ge(pool_chain, made[0])
                    pool.sem_inc(passed_pool, 1)

                def newton(i, u, r):
                    nt, mv = ntau[:, u % 2], move[:, u % 2]
                    if r == FIRST_ROUNDS - 1:
                        pool.wait_ge(inv_made, i + 1)
                    else:
                        pool.wait_ge(excess_made, ROUNDS * i + r + 1)
                    pool.sem_inc(passed_pool, 1)
                    link(G.tensor_tensor(over1[:], excess[:, u % 2, r], unit[:], ALU.subtract))
                    link(G.tensor_tensor(mv, over1[:], inv[:, u % 2], ALU.mult))
                    if r < ROUNDS - 1:
                        G.tensor_tensor(nt, nt, mv, ALU.subtract).then_inc(tau_tried_last, 1)
                        pool.wait_ge(tau_tried_last, (ROUNDS - FIRST_ROUNDS) * i + r - FIRST_ROUNDS + 2)
                        pool.sem_inc(passed_pool, 1)
                    else:
                        link(G.tensor_tensor(nt, nt, mv, ALU.subtract))
                        G.tensor_tensor(miss[:], over1[:], over1[:], ALU.mult).then_inc(stepped, 1)

                if has(i, 2):
                    newton(i - 2, (u - 2) % U, 3)
                    newton(i - 2, (u - 2) % U, 4)
                if has(i, 1):
                    e = excess[:, (u - 1) % 2]
                    pool.wait_ge(tau_tried, FIRST_ROUNDS * (i - 1) + 2)
                    pool.sem_inc(passed_pool, 1)
                    link(G.tensor_tensor(e_plus1[:], e[:, 0], unit[:], ALU.add))
                    link(G.tensor_tensor(e_plus1[:], e_plus1[:], per_count[:], ALU.mult))
                    link(G.tensor_scalar(e_bound[:], e[:, 0], 0.25, 4.0, ALU.max, ALU.min))
                    G.tensor_tensor(model[:], e_bound[:], e_plus1[:], ALU.mult).then_inc(model_made, 1)
                if has(i, 2):
                    nt = ntau[:, (u - 2) % 2]
                    pool.wait_ge(settled, i - 1)
                    pool.sem_inc(passed_pool, 1)
                    pool.wait_ge(tau_turned, i - 2)
                    pool.sem_inc(passed_pool, 1)
                    link(G.tensor_copy(split[:, :, 0], nt))
                    link(G.tensor_tensor(rest[:], nt, split[:, :, 0], ALU.subtract))
                    link(G.tensor_copy(split[:, :, 1], rest[:]))
                    G.tensor_tensor(split[:, :, 2], rest[:], split[:, :, 1], ALU.subtract).then_inc(tau_split, 1)
                if has(i, 1):
                    mv = move[:, (u - 1) % 2]
                    pool.wait_ge(excess_made, ROUNDS * (i - 1) + 3)
                    pool.sem_inc(passed_pool, 1)
                    G.tensor_tensor(square[:], mv, mv, ALU.mult)
                    link(G.tensor_tensor(fall[:], e[:, 1], e[:, 2], ALU.subtract))
                    G.tensor_tensor(fall[:], fall[:], mv, ALU.mult).then_inc(fall_made, 1)
                    newton(i - 1, (u - 1) % U, 2)

            walk(pool, step)


def experts_program(nc, x, g_attn, g_ffn, wo, bo, o_parts, router_w, w_in, b_in, w_out, b_out, ident_in, out):
    with ExitStack() as ctx:
        def sb(name, shape, dt=F32):
            return ctx.enter_context(nc.sbuf_tensor("e_" + name, shape, dt))

        def sem(name):
            return ctx.enter_context(nc.semaphore("e_" + name))

        def ps(name, banks):
            return ctx.enter_context(nc.psum_tensor("e_" + name, [P, banks, BANK], F32))

        hid_ps = ps("hid_ps", 4)
        y_ps = ps("y_ps", 2)
        turn_ps = ps("turn_ps", 2)
        p_tile = [turn_ps[:, t // 2, (t % 2) * DIM:(t % 2 + 1) * DIM] for t in range(TILES)]
        y_tile = [y_ps[:, t // 2, (t % 2) * DIM:(t % 2 + 1) * DIM] for t in range(TILES)]

        win_s = sb("w_in", [P, EXPERTS, HALVES, HIDDEN])
        wout_s = sb("w_out", [P, EXPERTS, HALVES, DIM])
        bin_s = sb("b_in", [P, EXPERTS, HALVES])
        bout_s = sb("b_out", [EXPERTS, DIM])
        wo_s = sb("wo", [P, HALVES, DIM])
        wr_s = sb("router", [P, HALVES, EXPERTS])
        bo_s = sb("bo", [P, DIM])
        ident = sb("ident", [P, P])
        g_s = sb("g", [P, 2])
        gates = sb("gates", [P, 2])
        places = sb("places", [P, EXPERTS])
        places_i = sb("places_i", [P, EXPERTS], I32)
        x_s = sb("x", [P, TILES, DIM])
        o_s = sb("o", [P, HALVES, 4, QUERIES])
        osum = sb("osum", [P, HALVES, QUERIES])
        x2_s = sb("x2", [P, 2, TILES, DIM])
        stats = sb("stats", [P, TILES, 6])
        moments = sb("moments", [P, TILES, 2])
        veps, std, rstd, fix = (sb(n, [P, TILES]) for n in ("veps", "std", "rstd", "fix"))
        xn = sb("xn", [P, TILES, DIM])
        xnt_s = sb("xnt", [P, 2, HALVES, QUERIES])
        logits = sb("logits", [P, TILES, EXPERTS])
        best = sb("best", [P, TILES, 8])
        best_i = sb("best_i", [P, TILES, 8], U32)
        best_f = sb("best_f", [P, TILES, 8])
        nbest = sb("nbest", [P, TILES])
        prob = sb("prob", [P, TILES, EXPERTS])
        mass = sb("mass", [P, TILES])
        rmass = sb("rmass", [P, TILES])
        pick = sb("pick", [P, TILES, EXPERTS])
        pick2 = sb("pick2", [P, TILES, EXPERTS])
        gate_s = sb("gate", [P, 2, TILES, EXPERTS])
        gate_t = sb("gate_t", [EXPERTS, QUERIES])
        hid = sb("hid", [P, 2, HALVES, QUERIES])
        acc = sb("acc", [P, TILES, DIM])
        res = sb("res", [P, TILES, DIM])

        weights, x_loaded, o_loaded, stored = sem("weights"), sem("x_loaded"), sem("o_loaded"), sem("stored")
        g_tanh = sem("g_tanh")
        places_made = sem("places_made")
        consts = sem("consts")
        chain = sem("chain")
        o_summed = sem("o_summed")
        projected = sem("projected")
        x2_done = sem("x2_done")
        stats_done = sem("stats_done")
        std_done = sem("std_done")
        normed = sem("normed")
        turned = sem("turned")
        xnt_done = sem("xnt_done")
        routed = sem("routed")
        best_done = sem("best_done")
        exp_done = sem("exp_done")
        gate_done = sem("gate_done")
        gate_turned = sem("gate_turned")
        gate_t_done = sem("gate_t_done")
        bias_made = sem("bias_made")
        hid_made = sem("hid_made")
        hid_done = sem("hid_done")
        y_made = sem("y_made")
        passed = sem("passed")
        y_used = sem("y_used")
        finished = sem("finished")
        LOADS = 9 + EXPERTS * HALVES

        block = ctx.enter_context(nc.Block())

        @block.sync
        def _(sp):
            sp.dma_start(win_s[:], w_in.rearrange("e (a p) n -> p e a n", p=P)).then_inc(weights, 16)
            sp.dma_start(wout_s[:], w_out.rearrange("e (a p) n -> p e a n", p=P)).then_inc(weights, 16)
            for e in range(EXPERTS):
                for a in range(HALVES):
                    sp.dma_start(bin_s[:, e, a:a + 1], b_in[e, a * P:(a + 1) * P].rearrange("(p o) -> p o", o=1)).then_inc(weights, 16)
            sp.dma_start(bout_s[:], b_out).then_inc(weights, 16)
            sp.dma_start(wo_s[:], wo.rearrange("(a p) n -> p a n", p=P)).then_inc(weights, 16)
            sp.dma_start(wr_s[:], router_w.rearrange("(a p) n -> p a n", p=P)).then_inc(weights, 16)
            sp.dma_start(bo_s[:], bo.rearrange("(o n) -> o n", o=1).broadcast_to([P, DIM])).then_inc(weights, 16)
            sp.dma_start(ident[:], ident_in).then_inc(weights, 16)
            for n, g in enumerate((g_attn, g_ffn)):
                sp.dma_start(g_s[:, n:n + 1], g.rearrange("(o n) -> o n", o=1).broadcast_to([P, 1])).then_inc(weights, 16)
            with sp.Fori(0, BATCH) as b:
                sp.wait_ge(x2_done, TILES * b)
                sp.dma_start(x_s[:], x[b].rearrange("(t p) d -> p t d", p=P)).then_inc(x_loaded, 16)
                for s in range(4):
                    sp.dma_start(o_s[:, :, s], o_parts[s, bass.ds(b * DIM, DIM)].rearrange("(a p) n -> p a n", p=P)).then_inc(o_loaded, 16)

        @block.gpsimd
        def _(pool):
            nc.gpsimd.iota(places_i[:], pattern=[[1, EXPERTS]], base=0, channel_multiplier=0).then_inc(places_made, 1)
            with pool.Fori(0, BATCH) as b:
                pool.wait_ge(finished, TILES * (b + 1))
                pool.dma_start(out[b].rearrange("(t p) d -> p t d", p=P), res[:]).then_inc(stored, 16)
            pool.wait_ge(stored, 16 * BATCH)

        def walk(engine, prepare, experts, stages):
            def batch(b, u, last=False):
                experts(b, u, (lambda k: None) if last else (lambda k: prepare(b + 1, 1 - u, k)))

            for k in range(stages):
                prepare(0, 0, k)
            with engine.Fori(0, (BATCH - 1) // 2) as g:
                for u in range(2):
                    batch(2 * g + u, u)
            for b in range((BATCH - 1) // 2 * 2, BATCH):
                batch(b, b % 2, b == BATCH - 1)

        @block.tensor
        def _(pe):
            pe.wait_ge(weights, 16 * LOADS)

            def prepare(b, u, k):
                if k == 0:
                    pe.wait_ge(gate_t_done, b)
                    pe.wait_ge(o_summed, b + 1)
                    for t in range(TILES):
                        for a in range(HALVES):
                            mm = nc.tensor.matmul(p_tile[t], osum[:, a, t * P:(t + 1) * P], wo_s[:, a], start=a == 0, stop=a == HALVES - 1, skip_group_check=True)
                    mm.then_inc(projected, 1)
                elif k == 1:
                    pe.wait_ge(normed, TILES * (b + 1))
                    for a in range(HALVES):
                        for t in range(TILES):
                            mm = nc.tensor.transpose(turn_ps[:, a, t * P:(t + 1) * P], xn[:, t, a * P:(a + 1) * P], ident[:])
                    mm.then_inc(turned, 1)
                else:
                    pe.wait_ge(xnt_done, HALVES * (b + 1))
                    for t in range(TILES):
                        for a in range(HALVES):
                            mm = nc.tensor.matmul(turn_ps[:, 0, t * EXPERTS:(t + 1) * EXPERTS], xnt_s[:, u, a, t * P:(t + 1) * P], wr_s[:, a], start=a == 0, stop=a == HALVES - 1, skip_group_check=True)
                    mm.then_inc(routed, 1)

            def experts(b, u, stage):
                def hidden(e):
                    for m in range(HALVES):
                        n = e * HALVES + m
                        pe.wait_ge(hid_done, HALVES * EXPERTS * b + (n - 2 * HALVES + 1 if n >= 2 * HALVES else 0))
                        for a in range(HALVES):
                            mm = nc.tensor.matmul(hid_ps[:, n % 4], win_s[:, e, a, m * P:(m + 1) * P], xnt_s[:, u, a], start=a == 0, stop=a == HALVES - 1)
                        mm.then_inc(hid_made, 1)

                hidden(0)
                pe.wait_ge(gate_done, b + 1)
                for t in range(TILES):
                    mm = nc.tensor.transpose(turn_ps[0:EXPERTS, 1, t * P:(t + 1) * P], gate_s[:, u, t], ident[:])
                mm.then_inc(gate_turned, 1)
                hidden(1)
                pe.wait_ge(gate_t_done, b + 1)
                pe.wait_ge(y_used, (EXPERTS + 1) * b)
                for t in range(TILES):
                    mm = nc.tensor.matmul(y_tile[t], gate_t[:, t * P:(t + 1) * P], bout_s[:], start=True, stop=True, skip_group_check=True)
                mm.then_inc(bias_made, 1)
                for e in range(EXPERTS):
                    pe.wait_ge(hid_done, HALVES * (EXPERTS * b + e + 1))
                    pe.wait_ge(y_used, (EXPERTS + 1) * b + e + 1)
                    for t in range(TILES):
                        for a in range(HALVES):
                            mm = nc.tensor.matmul(y_tile[t], hid[:, e % 2, a, t * P:(t + 1) * P], wout_s[:, e, a], start=a == 0, stop=a == HALVES - 1, skip_group_check=True)
                    mm.then_inc(y_made, 1)
                    if e + 2 < EXPERTS:
                        hidden(e + 2)
                    if e in (0, 3, 4):
                        stage((0, 3, 4).index(e))

            walk(pe, prepare, experts, 3)

        @block.scalar
        def _(act):
            act.wait_ge(weights, 16 * LOADS)
            nc.scalar.activation(gates[:], g_s[:], ACT.Tanh).then_inc(g_tanh, 1)

            def prepare(b, u, k):
                if k == 0:
                    act.wait_ge(stats_done, b + 1)
                    nc.scalar.activation(std[:], veps[:], ACT.Sqrt).then_inc(std_done, 1)
                else:
                    act.wait_ge(best_done, b + 1)
                    for t in range(TILES):
                        ins = nc.scalar.activation(prob[:, t], logits[:, t], ACT.Exp, bias=nbest[:, t:t + 1], accum_out=mass[:, t:t + 1])
                    ins.then_inc(exp_done, 1)

            def experts(b, u, stage):
                for e in range(EXPERTS):
                    for m in range(HALVES):
                        n = e * HALVES + m
                        act.wait_ge(hid_made, HALVES * EXPERTS * b + n + 1)
                        if m == 0:
                            act.wait_ge(y_made, EXPERTS * b + max(e - 1, 0))
                        nc.scalar.activation(hid[:, e % 2, m], hid_ps[:, n % 4], ACT.Gelu_apprx_tanh, bias=bin_s[:, e, m:m + 1]).then_inc(hid_done, 1)
                    if e in (3, 7):
                        stage((3, 7).index(e))

            walk(act, prepare, experts, 2)

        @block.vector
        def _(dve):
            V = nc.vector
            dve.wait_ge(weights, 16 * LOADS)
            dve.wait_ge(g_tanh, 1)
            dve.wait_ge(places_made, 1)
            V.tensor_copy(places[:], places_i[:]).then_inc(consts, 1)
            V.tensor_scalar(bo_s[:], bo_s[:], gates[:, 0:1], None, ALU.mult).then_inc(consts, 1)
            dve.wait_ge(consts, 2)
            STAGE_LINKS = [2 + 1, 2, 5, 0, 1 + 2 + 4, 2]

            def prepare(b, u, k):
                made = [b * sum(STAGE_LINKS) + sum(STAGE_LINKS[:k])]
                x2, xnt, gate = x2_s[:, u], xnt_s[:, u], gate_s[:, u]

                def link(ins):
                    made[0] = made[0] + 1
                    ins.then_inc(chain, 1)
                    dve.wait_ge(chain, made[0])

                if k == 0:
                    dve.wait_ge(o_loaded, 64 * (b + 1))
                    link(V.tensor_tensor(osum[:], o_s[:, :, 0], o_s[:, :, 1], ALU.add))
                    link(V.tensor_tensor(osum[:], osum[:], o_s[:, :, 2], ALU.add))
                    V.tensor_tensor(osum[:], osum[:], o_s[:, :, 3], ALU.add).then_inc(o_summed, 1)
                    dve.wait_ge(x_loaded, 16 * (b + 1))
                    for t in range(TILES):
                        ins = V.tensor_tensor(x2[:, t], x_s[:, t], bo_s[:], ALU.add)
                    link(ins)
                elif k == 1:
                    dve.wait_ge(projected, b + 1)
                    for t in range(TILES):
                        V.scalar_tensor_tensor(out=x2[:, t], in0=p_tile[t], scalar=gates[:, 0:1], in1=x2[:, t], op0=ALU.mult, op1=ALU.add).then_inc(x2_done, 1)
                    dve.wait_ge(x2_done, TILES * (b + 1))
                    for t in range(TILES):
                        ins = V.bn_stats(stats[:, t], x2[:, t])
                    link(ins)
                    dve.sem_inc(passed, 1)
                    for t in range(TILES):
                        ins = V.bn_aggr(moments[:, t], stats[:, t])
                    link(ins)
                    V.tensor_scalar(veps[:], moments[:, :, 1], EPS, None, ALU.add).then_inc(stats_done, 1)
                elif k == 2:
                    dve.wait_ge(std_done, b + 1)
                    link(V.reciprocal(rstd[:], std[:]))
                    link(V.tensor_tensor(fix[:], rstd[:], rstd[:], ALU.mult))
                    link(V.tensor_tensor(fix[:], fix[:], veps[:], ALU.mult))
                    link(V.tensor_scalar(fix[:], fix[:], -0.5, 1.5, ALU.mult, ALU.add))
                    link(V.tensor_tensor(rstd[:], rstd[:], fix[:], ALU.mult))
                    for t in range(TILES):
                        V.tensor_scalar(xn[:, t], x2[:, t], moments[:, t, 0:1], rstd[:, t:t + 1], ALU.subtract, ALU.mult).then_inc(normed, 1)
                elif k == 3:
                    dve.wait_ge(turned, b + 1)
                    for a in range(HALVES):
                        V.tensor_copy(xnt[:, a], turn_ps[:, a]).then_inc(xnt_done, 1)
                elif k == 4:
                    dve.wait_ge(routed, b + 1)
                    link(V.tensor_copy(logits[:], turn_ps[:, 0, 0:TILES * EXPERTS].rearrange("p (t e) -> p t e", t=TILES)))
                    dve.sem_inc(passed, 1)
                    for t in range(TILES):
                        ins = V.max(best[:, t], logits[:, t])
                    link(ins)
                    V.tensor_scalar(nbest[:], best[:, :, 0], -1.0, None, ALU.mult).then_inc(best_done, 1)
                    for t in range(TILES):
                        ins = V.max_index(best_i[:, t], best[:, t], logits[:, t])
                    link(ins)
                    link(V.tensor_copy(best_f[:], best_i[:]))
                    every = places[:].unsqueeze(1).broadcast_to([P, TILES, EXPERTS])
                    link(V.tensor_tensor(pick[:], every, best_f[:, :, 0:1].broadcast_to([P, TILES, EXPERTS]), ALU.is_equal))
                    link(V.tensor_tensor(pick2[:], every, best_f[:, :, 1:2].broadcast_to([P, TILES, EXPERTS]), ALU.is_equal))
                    link(V.tensor_tensor(pick[:], pick[:], pick2[:], ALU.add))
                else:
                    dve.wait_ge(exp_done, b + 1)
                    link(V.reciprocal(rmass[:], mass[:]))
                    link(V.tensor_tensor(pick[:], pick[:], prob[:], ALU.mult))
                    V.tensor_tensor(gate, pick[:], rmass[:].unsqueeze(2).broadcast_to([P, TILES, EXPERTS]), ALU.mult).then_inc(gate_done, 1)

            def experts(b, u, stage):
                dve.wait_ge(gate_turned, b + 1)
                V.tensor_copy(gate_t[:], turn_ps[0:EXPERTS, 1]).then_inc(gate_t_done, 1)
                dve.wait_ge(bias_made, b + 1)
                for t in range(TILES):
                    ins = V.tensor_copy(acc[:, t], y_tile[t])
                ins.then_inc(y_used, 1)
                stage(0)
                for e in range(EXPERTS):
                    dve.wait_ge(y_made, EXPERTS * b + e + 1)
                    dve.wait_ge(y_used, (EXPERTS + 1) * b + e + 1)
                    for t in range(TILES):
                        ins = V.scalar_tensor_tensor(out=acc[:, t], in0=y_tile[t], scalar=gate_s[:, u, t, e:e + 1], in1=acc[:, t], op0=ALU.mult, op1=ALU.add)
                    ins.then_inc(y_used, 1)
                    if e in (1, 2, 3, 4, 6):
                        stage(1 + (1, 2, 3, 4, 6).index(e))
                dve.wait_ge(y_used, (EXPERTS + 1) * (b + 1))
                dve.wait_ge(stored, 16 * b)
                for t in range(TILES):
                    V.scalar_tensor_tensor(out=res[:, t], in0=acc[:, t], scalar=gates[:, 1:2], in1=x2_s[:, u, t], op0=ALU.mult, op1=ALU.add).then_inc(finished, 1)

            walk(dve, prepare, experts, 6)


def program(nc, x, ctx_t, ident, g_xattn, g_ffn, wq, bq, wk, bk, wv, bv, wo, bo, router_w, w_in, b_in, w_out, b_out, out):
    q_parts = nc.dram_tensor("q_parts", (3, BATCH * DIM, QUERIES), BF16).ap()
    k_parts = nc.dram_tensor("k_parts", (3, BATCH * DIM, KEYS), BF16).ap()
    v_heads = nc.dram_tensor("v_heads", (BATCH * HEADS, P, KCHUNKS, HEAD_DIM), F32).ap()
    o_parts = nc.dram_tensor("o_parts", (4, BATCH * DIM, QUERIES), F32).ap()
    project_program(nc, x, ctx_t, wq, bq, wk, bk, wv, bv, ident, q_parts, k_parts, v_heads)
    attend_program(nc, q_parts, k_parts, v_heads, ident, o_parts)
    experts_program(nc, x, g_xattn, g_ffn, wo, bo, o_parts, router_w, w_in, b_in, w_out, b_out, ident, out)


_INS = ["x", "ctx_t", "ident", "g_xattn", "g_ffn", "L0_xattn_Wq", "L0_xattn_bq", "L0_xattn_Wk", "L0_xattn_bk",
        "L0_xattn_Wv", "L0_xattn_bv", "L0_xattn_Wo", "L0_xattn_bo", "L0_ffn_router_w", "L0_ffn_w_in", "L0_ffn_b_in",
        "L0_ffn_w_out", "L0_ffn_b_out"]


def kernel(**inputs):
    import numpy as np
    import concourse.bacc as bacc
    from concourse.bass_utils import run_bass_kernel_spmd

    nc = bacc.Bacc("TRN2", target_bir_lowering=False, num_devices=1)
    laid = dict(inputs)
    laid["ctx_t"] = np.transpose(np.asarray(inputs["ctx_1024"]), (0, 2, 1))
    laid["ident"] = np.eye(P, dtype=np.float32)
    arrays, args = {}, []
    for name in _INS:
        a = np.ascontiguousarray(laid[name])
        arrays[f"in_{name}"] = a
        args.append(nc.dram_tensor(f"in_{name}", a.shape, mybir.dt.from_np(a.dtype), kind="ExternalInput").ap())
    out = nc.dram_tensor("out_0", (BATCH, QUERIES, DIM), F32, kind="ExternalOutput").ap()
    program(nc, *args, out)
    r = run_bass_kernel_spmd(nc, [arrays], core_ids=[0])
    return r.results[0]["out_0"]
```
